# Optimizing a Trainium2 kernel written in Bass

```python
import numpy as np
import jax
import jax.numpy as jnp

def _softmax(x, axis=-1):
    return jax.nn.softmax(x, axis=axis)

def _gelu(x):
    return jax.nn.gelu(x, approximate=True)

def _silu(x):
    return jax.nn.silu(x)

def _sigmoid(x):
    return jax.nn.sigmoid(x)

def _layernorm(x, axis=-1, eps=1e-05):
    m = jnp.mean(x, axis=axis, keepdims=True)
    v = jnp.var(x, axis=axis, keepdims=True)
    return (x - m) / jnp.sqrt(v + eps)

def _scatter_add(tgt, idx, src, axis=0):
    return tgt.at[idx].add(src)

def _segment_sum(src, seg, n):
    return jax.ops.segment_sum(src, seg, n)
kernel_name = 'mk_gnn_ffn_d2_gnn_r8_53e2af'

def setup_inputs(seed: int=0):
    np.random.seed(seed)
    _w = jnp.asarray

    def _rec_inputs():
        import jax
        import jax.numpy as jnp
        _gk = jax.random.key(seed)
        x = -0.0003713 + 1 * jax.random.normal(jax.random.fold_in(_gk, 1), (6250, 256), jnp.float32)
        src = jax.random.randint(jax.random.fold_in(_gk, 2), (200000,), 0, 6250, jnp.int32)
        dst = jax.random.randint(jax.random.fold_in(_gk, 3), (200000,), 0, 6250, jnp.int32)
        _o = jnp.argsort(dst, stable=True)
        src = src[_o]
        dst = dst[_o]
        return (x, src, dst)
    x, src, dst = _rec_inputs()

    def _L0_gnn_setup():
        import jax, jax.numpy as jnp
        import numpy as np
        N_NODES = 6250
        N_EDGES = 100000
        IN_SIZE = 256
        OUT_SIZE = 256
        key = jax.random.key(seed)
        kx, ks, kd, kw, kb = jax.random.split(key, 5)
        x = jax.random.normal(kx, (N_NODES, IN_SIZE), dtype=jnp.float32)
        src_rand = jax.random.randint(ks, (N_EDGES - N_NODES,), 0, N_NODES)
        src = jnp.concatenate([jnp.arange(N_NODES), src_rand]).astype(jnp.int64)
        dst = jax.random.randint(kd, (N_EDGES,), 0, N_NODES).astype(jnp.int64)
        edge_index = jnp.stack([src, dst])
        bound = 1.0 / np.sqrt(IN_SIZE)
        W = jax.random.uniform(kw, (OUT_SIZE, IN_SIZE), dtype=jnp.float32, minval=-bound, maxval=bound)
        b = jax.random.uniform(kb, (OUT_SIZE,), dtype=jnp.float32, minval=-bound, maxval=bound)
        return {'x': x, 'edge_index': edge_index, 'W': W, 'b': b}
    _L0_gnn_all = _L0_gnn_setup()
    _L0_gnn_in = {k: v for k, v in _L0_gnn_all.items() if k in ('W', 'b')}
    del _L0_gnn_all

    def _L0_ffn_setup():
        import math
        import jax, jax.numpy as jnp
        import numpy as np
        CAPACITY_FACTOR = 1.25
        TOP_K = 2
        LN_EPS = 1e-05

        def _layer_norm(x, gamma, beta):
            mu = jnp.mean(x, axis=-1, keepdims=True)
            var = jnp.var(x, axis=-1, keepdims=True)
            return (x - mu) * jax.lax.rsqrt(var + LN_EPS) * gamma + beta
        key = jax.random.key(seed)
        ks = jax.random.split(key, 4)
        B, S, D, F, E = (8, 512, 256, 512, 8)
        x = jax.random.normal(ks[0], (B, S, D), dtype=jnp.float32)
        Wr = jax.random.normal(ks[1], (D, E), dtype=jnp.float32) / np.sqrt(D)
        br = jnp.zeros((E,), jnp.float32)
        W1 = jax.random.normal(ks[2], (E, D, F), dtype=jnp.float32) / np.sqrt(D)
        b1 = jnp.zeros((E, F), jnp.float32)
        W2 = jax.random.normal(ks[3], (E, F, D), dtype=jnp.float32) / np.sqrt(F)
        b2 = jnp.zeros((E, D), jnp.float32)
        gamma = jnp.ones((D,), jnp.float32)
        beta = jnp.zeros((D,), jnp.float32)
        return {'x': x, 'Wr': Wr, 'br': br, 'W1': W1, 'b1': b1, 'W2': W2, 'b2': b2, 'gamma': gamma, 'beta': beta}
    _L0_ffn_all = _L0_ffn_setup()
    _L0_ffn_in = {k: v for k, v in _L0_ffn_all.items() if k in ('Wr', 'br', 'W1', 'b1', 'W2', 'b2', 'gamma', 'beta')}
    del _L0_ffn_all

    def _L1_gnn_setup():
        import jax, jax.numpy as jnp
        import numpy as np
        NEG_SLOPE = 0.2
        N_NODES = 6250
        N_EDGES = 100000

        def gat_conv(h, src, dst, W, al, ar, residual):
            N = h.shape[0]
            H, D = al.shape
            feat = (h @ W).reshape(N, H, D)
            el = jnp.sum(feat * al, axis=-1)
            er = jnp.sum(feat * ar, axis=-1)
            e = jax.nn.leaky_relu(el[src] + er[dst], NEG_SLOPE)
            emax = jax.ops.segment_max(e, dst, num_segments=N)
            ex = jnp.exp(e - emax[dst])
            denom = jax.ops.segment_sum(ex, dst, num_segments=N)
            a = ex / denom[dst]
            msg = feat[src] * a[:, :, None]
            rst = jax.ops.segment_sum(msg, dst, num_segments=N)
            if residual:
                rst = rst + h.reshape(N, H, D)
            return jax.nn.elu(rst).reshape(N, H * D)
        key = jax.random.key(seed)
        ks = jax.random.split(key, 9)
        features = jax.random.normal(ks[0], (N_NODES, 256), dtype=jnp.float32)
        src = jax.random.randint(ks[1], (N_EDGES,), 0, N_NODES, dtype=jnp.int32)
        dst = jax.random.randint(ks[2], (N_EDGES,), 0, N_NODES, dtype=jnp.int32)
        s1 = 1.0 / np.sqrt(256.0)
        W1 = jax.random.normal(ks[3], (256, 256), dtype=jnp.float32) * s1
        al1 = jax.random.normal(ks[4], (4, 64), dtype=jnp.float32) * 0.1
        ar1 = jax.random.normal(ks[5], (4, 64), dtype=jnp.float32) * 0.1
        W2 = jax.random.normal(ks[6], (256, 256), dtype=jnp.float32) * s1
        al2 = jax.random.normal(ks[7], (4, 64), dtype=jnp.float32) * 0.1
        ar2 = jax.random.normal(ks[8], (4, 64), dtype=jnp.float32) * 0.1
        return {'features': features, 'src': src, 'dst': dst, 'W1': W1, 'al1': al1, 'ar1': ar1, 'W2': W2, 'al2': al2, 'ar2': ar2}
    _L1_gnn_all = _L1_gnn_setup()
    _L1_gnn_in = {k: v for k, v in _L1_gnn_all.items() if k in ('W1', 'al1', 'ar1', 'W2', 'al2', 'ar2')}
    del _L1_gnn_all

    def _L1_ffn_setup():
        import jax, jax.numpy as jnp
        import numpy as np
        IN_CH = 256
        OUT_CH = 256
        key = jax.random.key(seed)
        kx, kw, kb = jax.random.split(key, 3)
        x = jax.random.normal(kx, (8, 512, IN_CH), dtype=jnp.float32)
        bound = 1.0 / np.sqrt(IN_CH)
        weight = jax.random.uniform(kw, (OUT_CH, IN_CH), dtype=jnp.float32, minval=-bound, maxval=bound)
        bias = jax.random.uniform(kb, (OUT_CH,), dtype=jnp.float32, minval=-bound, maxval=bound)
        return {'x': x, 'weight': weight, 'bias': bias}
    _L1_ffn_all = _L1_ffn_setup()
    _L1_ffn_in = {k: v for k, v in _L1_ffn_all.items() if k in ('weight', 'bias')}
    del _L1_ffn_all
    return {'x': x, 'src': src, 'dst': dst, 'L0_gnn_W': _L0_gnn_in['W'], 'L0_gnn_b': _L0_gnn_in['b'], 'L0_ffn_Wr': _L0_ffn_in['Wr'], 'L0_ffn_br': _L0_ffn_in['br'], 'L0_ffn_W1': _L0_ffn_in['W1'], 'L0_ffn_b1': _L0_ffn_in['b1'], 'L0_ffn_W2': _L0_ffn_in['W2'], 'L0_ffn_b2': _L0_ffn_in['b2'], 'L0_ffn_gamma': _L0_ffn_in['gamma'], 'L0_ffn_beta': _L0_ffn_in['beta'], 'L1_gnn_W1': _L1_gnn_in['W1'], 'L1_gnn_al1': _L1_gnn_in['al1'], 'L1_gnn_ar1': _L1_gnn_in['ar1'], 'L1_gnn_W2': _L1_gnn_in['W2'], 'L1_gnn_al2': _L1_gnn_in['al2'], 'L1_gnn_ar2': _L1_gnn_in['ar2'], 'L1_ffn_weight': _L1_ffn_in['weight'], 'L1_ffn_bias': _L1_ffn_in['bias']}

def reference(x, src, dst, L0_gnn_W, L0_gnn_b, L0_ffn_Wr, L0_ffn_br, L0_ffn_W1, L0_ffn_b1, L0_ffn_W2, L0_ffn_b2, L0_ffn_gamma, L0_ffn_beta, L1_gnn_W1, L1_gnn_al1, L1_gnn_ar1, L1_gnn_W2, L1_gnn_al2, L1_gnn_ar2, L1_ffn_weight, L1_ffn_bias):
    import jax
    import jax.numpy as jnp

    def _L0_gnn_ref(x, edge_index, W, b):
        import jax, jax.numpy as jnp
        import numpy as np
        N_NODES = 6250
        N_EDGES = 100000
        IN_SIZE = 256
        OUT_SIZE = 256
        N = x.shape[0]
        src, dst = (edge_index[0], edge_index[1])
        deg = jnp.zeros((N,), dtype=x.dtype).at[src].add(1.0)
        dinv = deg ** (-0.5)
        loop = jnp.arange(N, dtype=src.dtype)
        src_sl = jnp.concatenate([src, loop])
        dst_sl = jnp.concatenate([dst, loop])
        coef = dinv[src_sl] * dinv[dst_sl]
        msg = x[dst_sl] * coef[:, None]
        agg = jax.ops.segment_sum(msg, src_sl, num_segments=N)
        return jax.nn.relu(agg @ W.T + b)

    def _L0_ffn_ref(x, Wr, br, W1, b1, W2, b2, gamma, beta):
        import math
        import jax, jax.numpy as jnp
        import numpy as np
        CAPACITY_FACTOR = 1.25
        TOP_K = 2
        LN_EPS = 1e-05

        def _layer_norm(x, gamma, beta):
            mu = jnp.mean(x, axis=-1, keepdims=True)
            var = jnp.var(x, axis=-1, keepdims=True)
            return (x - mu) * jax.lax.rsqrt(var + LN_EPS) * gamma + beta
        B, S, D = x.shape
        E = Wr.shape[1]
        N = B * S
        K = TOP_K
        logits = jnp.mean(x, axis=1) @ Wr + br
        routing_weights = jax.nn.softmax(logits, axis=-1)
        capacity = float(math.ceil(N * CAPACITY_FACTOR / E))
        expected_loads = routing_weights.sum(axis=0) * (N / B)
        scale = jnp.where(expected_loads > capacity, capacity / expected_loads, 1.0)
        routing_weights = jax.nn.softmax(routing_weights * scale, axis=-1)
        rw_tok = jnp.broadcast_to(routing_weights[:, None, :], (B, S, E)).reshape(N, E)
        top_w, top_i = jax.lax.top_k(rw_tok, K)
        top_w = jax.nn.softmax(top_w, axis=-1)
        xf = x.reshape(N, D)
        h = jax.nn.gelu(jnp.einsum('nd,edf->enf', xf, W1) + b1[:, None, :], approximate=False)
        y = jnp.einsum('enf,efd->end', h, W2) + b2[:, None, :]
        w_dense = jnp.zeros((N, E), x.dtype).at[jnp.arange(N)[:, None], top_i].add(top_w)
        out = jnp.einsum('ne,end->nd', w_dense, y).reshape(B, S, D)
        out = _layer_norm(out + x, gamma, beta)
        return out

    def _L1_gnn_ref(features, src, dst, W1, al1, ar1, W2, al2, ar2):
        import jax, jax.numpy as jnp
        import numpy as np
        NEG_SLOPE = 0.2
        N_NODES = 6250
        N_EDGES = 100000

        def gat_conv(h, src, dst, W, al, ar, residual):
            N = h.shape[0]
            H, D = al.shape
            feat = (h @ W).reshape(N, H, D)
            el = jnp.sum(feat * al, axis=-1)
            er = jnp.sum(feat * ar, axis=-1)
            e = jax.nn.leaky_relu(el[src] + er[dst], NEG_SLOPE)
            emax = jax.ops.segment_max(e, dst, num_segments=N)
            ex = jnp.exp(e - emax[dst])
            denom = jax.ops.segment_sum(ex, dst, num_segments=N)
            a = ex / denom[dst]
            msg = feat[src] * a[:, :, None]
            rst = jax.ops.segment_sum(msg, dst, num_segments=N)
            if residual:
                rst = rst + h.reshape(N, H, D)
            return jax.nn.elu(rst).reshape(N, H * D)
        h = gat_conv(features, src, dst, W1, al1, ar1, residual=False)
        h = gat_conv(h, src, dst, W2, al2, ar2, residual=True)
        return h

    def _L1_ffn_ref(x, weight, bias):
        import jax, jax.numpy as jnp
        import numpy as np
        IN_CH = 256
        OUT_CH = 256
        return jnp.einsum('bsi,oi->bso', x, weight) + bias
    edge_index = jnp.stack([src, dst])
    x = x + _L0_gnn_ref(_layernorm(x, axis=-1), edge_index, L0_gnn_W, L0_gnn_b)
    x = x + _L0_ffn_ref(_layernorm(x, axis=-1)[None], L0_ffn_Wr, L0_ffn_br, L0_ffn_W1, L0_ffn_b1, L0_ffn_W2, L0_ffn_b2, L0_ffn_gamma, L0_ffn_beta)[0]
    x = x + _L1_gnn_ref(_layernorm(x, axis=-1), src, dst, L1_gnn_W1, L1_gnn_al1, L1_gnn_ar1, L1_gnn_W2, L1_gnn_al2, L1_gnn_ar2)
    x = x + _L1_ffn_ref(_layernorm(x, axis=-1)[None], L1_ffn_weight, L1_ffn_bias)[0]
    return x

_drawn_inputs = setup_inputs


def setup_inputs(seed=0):
    import zlib

    import numpy as np

    out = dict(_drawn_inputs(seed))
    spreads = {'L0_ffn_br': (0.0, 0.8),
     'L0_ffn_b1': (0.0, 0.343),
     'L0_ffn_b2': (0.0, 0.1),
     'L0_ffn_gamma': (1.0, 0.2),
     'L0_ffn_beta': (0.0, 0.1)}
    factors = {'L0_ffn_Wr': 8.0,
     'L1_gnn_ar1': 2.989,
     'L1_gnn_al2': 8.0,
     'L1_gnn_ar2': 8.0,
     'L1_ffn_bias': 3.117}
    for name, (base, spread) in spreads.items():
        noise = np.random.default_rng([zlib.crc32(name.encode()), seed]).standard_normal(out[name].shape)
        drawn = base * np.exp(spread * noise) if base else spread * noise
        out[name] = jnp.asarray(drawn.astype(out[name].dtype))
    for name, factor in factors.items():
        out[name] = (out[name] * factor).astype(out[name].dtype)
    return out
```

```python
from contextlib import ExitStack

import concourse.bass as bass
from concourse import mybir

FP32, BF16, I32, U32 = mybir.dt.float32, mybir.dt.bfloat16, mybir.dt.int32, mybir.dt.uint32
ALU = mybir.AluOpType
ACT = mybir.ActivationFunctionType
AX = mybir.AxisListType
ET = mybir.EngineType

P = 128
N, D, E = 6250, 256, 200000
NBLK = -(-N // P)
NB = NBLK + 1
N_PAD = NB * P
HEADS, HD = 4, 64
GROUP = 4
SLOTS = 4
BODY = GROUP * SLOTS
N_WIN = -(-(E // P + 1 + NBLK) // BODY) * BODY
N_IT = N_WIN // BODY
WPP = -(-N_WIN // P)
WL = WPP * P
LINE = WPP * P
EDGE_ROWS = E // P + 4
START_MAX = E + 64
FAR = 8191.0
BIG = 1.0e30
RING = 2
MADE, ROOM = RING + 1, 1
RAW_P, RAW_C = 125, E // 125
EPS = 1e-5
TAIL = N - (NBLK - 1) * P
ROW = D + HEADS


class Shared:
    pass


class Tables:
    pass


class Steps:

    def __init__(self, engine, sem):
        self.engine, self.sem, self.n = engine, sem, 0

    def mark(self, ins):
        self.n += 1
        ins.then_inc(self.sem, 1)

    def then(self, ins):
        self.mark(ins)
        self.engine.wait_ge(self.sem, self.n)

    def wait(self):
        self.engine.wait_ge(self.sem, self.n)


def scope(nc, stage):
    ctx = ExitStack()
    sems = []

    def sem(name):
        sems.append(nc.alloc_semaphore(name=f"{stage}_{name}"))
        return sems[-1]

    def clear():
        with nc.Block() as block:

            @block.gpsimd
            def _(pool):
                nc.clear_and_free_semaphores(sems)

    sb = lambda name, shape, dt=FP32: ctx.enter_context(nc.sbuf_tensor(f"{stage}_{name}", shape, dt))
    ctx.callback(clear)
    return ctx, sb, sem


def bc(ap, shape):
    return ap.to_broadcast(shape)


def constants(nc, S):
    ctx, sb, sem = scope(nc, "const")
    with ctx:
        made, cast = sem("made"), sem("cast")
        with nc.Block() as block:

            @block.gpsimd
            def _(pool):
                st = Steps(pool, made)
                st.mark(nc.gpsimd.memset(S.ident[:], 0.0))
                st.mark(nc.gpsimd.memset(S.ones[:], 1.0))
                st.mark(nc.gpsimd.memset(S.lower[:], 1.0))
                st.mark(nc.gpsimd.iota(S.row[:], pattern=[[1, P]], base=0, channel_multiplier=0,
                                       allow_small_or_imprecise_dtypes=True))
                st.then(nc.gpsimd.iota(S.col[:], pattern=[[0, 1]], base=0, channel_multiplier=1,
                                       allow_small_or_imprecise_dtypes=True))
                st.mark(nc.gpsimd.affine_select(out=S.ident[:], in_=S.ident[:], compare_op=ALU.not_equal, fill=1.0,
                                                base=0, pattern=[[-1, P]], channel_multiplier=1))
                st.then(nc.gpsimd.affine_select(out=S.lower[:], in_=S.lower[:], compare_op=ALU.is_gt, fill=0.0,
                                                base=0, pattern=[[-1, P]], channel_multiplier=1))

            @block.vector
            def _(dve):
                dve.wait_ge(made, 7)
                nc.vector.tensor_copy(S.ident_b[:], S.ident[:]).then_inc(cast, 1)
                nc.vector.tensor_copy(S.lower_b[:], S.lower[:]).then_inc(cast, 1)
                nc.vector.tensor_copy(S.row_b[:], S.row[:]).then_inc(cast, 1)
                nc.vector.tensor_scalar(S.minus_col[:], S.col[:], -1.0, None, ALU.mult).then_inc(cast, 1)
                dve.wait_ge(cast, 4)


def prep_edges(nc, S, T, src, dst):
    ctx, sb, sem = scope(nc, "prep")
    with ctx:
        dst_i = sb("dst_i", [P, RAW_C], I32)
        dst_b = sb("dst_b", [P, RAW_C], BF16)
        junk = sb("junk", [P, RAW_C], BF16)
        thr = sb("thr", [P, NB])
        cnt = sb("cnt", [P, NB])
        pads = sb("pads", [8, 2, (EDGE_ROWS * P - E) // 8], I32)
        bs = sb("bs", [P, NB])
        nw = sb("nw", [P, NBLK])
        nwi = sb("nwi", [P, NBLK], I32)
        ws = sb("ws", [P, NB])
        zero = sb("zero", [P, LINE])
        off = sb("off", [P, NB])
        dof = sb("dof", [P, NBLK])
        wid = sb("wid", [P, WPP])
        cmp = sb("cmp", [P, WPP, NBLK])
        blk = sb("blk", [P, WPP])
        start = sb("start", [P, WPP])
        idx = sb("idx", [P, WPP], I32)
        blki = sb("blki", [P, WPP], I32)
        line_i = sb("line_i", [P, 2, LINE], I32)
        ls = sb("ls", [P, LINE])
        rel = sb("rel", [P, LINE])
        valid = sb("valid", [P, LINE])
        bw = sb("bw", [P, LINE])
        tmp = sb("tmp", [P, WL], I32)
        loaded, padded, dved = sem("loaded"), sem("padded"), sem("dve")
        dstd, counted, summed = sem("dstd"), sem("counted"), sem("summed")
        indexed, gathered, blocks = sem("indexed"), sem("gathered"), sem("blocks")
        lines, turned, taken = sem("lines"), sem("turned"), sem("taken")
        made, blkout, cnts = sem("made"), sem("blkout"), sem("cnts")

        with nc.Block() as block:

            @block.sync
            def _(sp):
                sp.dma_start(dst_i[0:RAW_P, :], dst.rearrange("(p c) -> p c", p=RAW_P)).then_inc(dstd, 16)
                for k, v in enumerate((src, dst)):
                    sp.dma_start(T.edges[k][0:E].rearrange("(p c) -> p c", p=RAW_P),
                                 v.rearrange("(p c) -> p c", p=RAW_P)).then_inc(loaded, 16)
                sp.wait_ge(made, 3)
                for k in range(2):
                    sp.dma_start(T.edges[k][E:EDGE_ROWS * P].rearrange("(p c) -> p c", p=8),
                                 pads[:, k, :]).then_inc(padded, 16)
                sp.wait_ge(blocks, 1)
                sp.dma_start(T.blk.rearrange("(p j) -> p j", j=WPP), blki[:]).then_inc(blkout, 16)
                sp.wait_ge(blkout, 16)
                sp.dma_start(S.blk_row[0:1, :], T.blk.rearrange("(a w) -> a w", a=1)).then_inc(blkout, 16)
                sp.wait_ge(blkout, 32)

            @block.gpsimd
            def _(pool):
                nc.gpsimd.memset(pads[:, 0, :], 0).then_inc(made, 1)
                nc.gpsimd.memset(pads[:, 1, :], int(FAR)).then_inc(made, 1)
                nc.gpsimd.iota(thr[:], pattern=[[1, NB]], base=0, channel_multiplier=0,
                               allow_small_or_imprecise_dtypes=True).then_inc(made, 1)
                nc.gpsimd.iota(wid[:], pattern=[[1, WPP]], base=0, channel_multiplier=WPP,
                               allow_small_or_imprecise_dtypes=True).then_inc(made, 1)
                nc.gpsimd.memset(zero[:], 0.0).then_inc(made, 1)
                pool.wait_ge(loaded, 32)
                pool.wait_ge(padded, 32)
                pool.wait_ge(indexed, 1)
                for k in range(2):
                    table = T.edges[k].rearrange("(r c) -> r c", c=P)
                    for j in range(WPP):
                        nc.gpsimd.indirect_dma_start(
                            out=line_i[:, k, j * P:(j + 1) * P], out_offset=None, in_=table,
                            in_offset=bass.IndirectOffsetOnAxis(ap=idx[:, j:j + 1].bitcast(U32), axis=1),
                        ).then_inc(gathered, 16)

            @block.vector
            def _(dve):
                st = Steps(dve, dved)
                V = nc.vector
                dve.wait_ge(dstd, 16)
                dve.wait_ge(made, 5)
                V.memset(cnt[:], 0.0).then_inc(cnts, 1)
                st.then(V.tensor_scalar(dst_i[0:RAW_P, :], dst_i[0:RAW_P, :], 7, None, ALU.arith_shift_right))
                st.then(V.tensor_copy(dst_b[0:RAW_P, :], dst_i[0:RAW_P, :]))
                with dve.Fori(1, NB) as b:
                    dve.wait_ge(cnts, b)
                    V.tensor_scalar(junk[0:RAW_P, :], dst_b[0:RAW_P, :], thr[0:RAW_P, bass.ds(b, 1)], 0.0,
                                    ALU.is_lt, ALU.add, accum_out=cnt[0:RAW_P, bass.ds(b, 1)]).then_inc(cnts, 1)
                dve.wait_ge(cnts, NB)
                V.memset(off[:], 0.0).then_inc(counted, 1)
                dve.wait_ge(counted, 1)
                dve.wait_ge(summed, 1)
                st.then(V.tensor_copy(bs[:], S.bank[0][:, 0:NB]))
                st.then(V.tensor_tensor(nw[:], bs[:, 1:NB], bs[:, 0:NBLK], ALU.subtract))
                st.then(V.tensor_scalar(nw[:], nw[:], float(P - 1), None, ALU.add))
                st.then(V.tensor_copy(nwi[:], nw[:]))
                st.then(V.tensor_scalar(nwi[:], nwi[:], 7, None, ALU.arith_shift_right))
                st.then(V.tensor_copy(nw[:], nwi[:]))
                st.mark(V.memset(ws[:, 0:1], 0.0))
                st.then(V.tensor_tensor_scan(ws[:, 1:NB], zero[:, 0:NBLK], nw[:], 0.0, ALU.add, ALU.add))
                st.then(V.scalar_tensor_tensor(out=off[:], in0=ws[:], scalar=-float(P), in1=bs[:],
                                               op0=ALU.mult, op1=ALU.add))
                st.then(V.tensor_tensor(dof[:], off[:, 1:NB], off[:, 0:NBLK], ALU.subtract))
                shape = [P, WPP, NBLK]
                st.then(V.tensor_tensor(cmp[:], bc(ws[:, None, 1:NB], shape), bc(wid[:, :, None], shape), ALU.is_le))
                st.then(V.tensor_reduce(blk[:], cmp[:], AX.X, ALU.add))
                st.then(V.tensor_tensor(cmp[:], cmp[:], bc(dof[:, None, :], shape), ALU.mult))
                st.then(V.tensor_reduce(start[:], cmp[:], AX.X, ALU.add))
                st.then(V.scalar_tensor_tensor(out=start[:], in0=wid[:], scalar=float(P), in1=start[:],
                                               op0=ALU.mult, op1=ALU.add))
                st.then(V.tensor_scalar(start[:], start[:], float(START_MAX), None, ALU.min))
                V.tensor_copy(idx[:], start[:]).then_inc(indexed, 1)
                V.tensor_copy(blki[:], blk[:]).then_inc(blocks, 1)
                shape = [P, WPP, P]
                st.then(V.tensor_copy(bw[:].rearrange("p (j e) -> p j e", e=P), bc(blk[:, :, None], shape)))
                dve.wait_ge(gathered, 2 * 16 * WPP)
                st.mark(V.tensor_copy(ls[:], line_i[:, 0, :]))
                st.then(V.tensor_copy(S.key[:], line_i[:, 1, :]))
                st.then(V.scalar_tensor_tensor(out=rel[:], in0=bw[:], scalar=-float(P), in1=S.key[:],
                                               op0=ALU.mult, op1=ALU.add))
                st.mark(V.tensor_scalar(valid[:], rel[:], 0.0, None, ALU.is_ge))
                st.then(V.tensor_scalar(bw[:], rel[:], float(P), None, ALU.is_lt))
                st.then(V.tensor_tensor(valid[:], valid[:], bw[:], ALU.mult))
                for x, out in ((S.key, S.key), (rel, rel), (ls, bw)):
                    st.then(V.scalar_tensor_tensor(out=out[:], in0=x[:], scalar=1.0, in1=valid[:],
                                                   op0=ALU.add, op1=ALU.mult))
                    st.then(V.tensor_scalar(out[:], out[:], -1.0, None, ALU.add))
                V.memset(off[:], 0.0).then_inc(lines, 1)
                for n in range(3 * WPP):
                    k, j = divmod(n, WPP)
                    dve.wait_ge(turned, n + 1)
                    to = (S.src_i, S.rel, S.src_m)[k]
                    V.tensor_copy(to[:].rearrange("e (p j) -> e j p", j=WPP)[:, j, :],
                                  S.bank[1 + n % 7][:, 0:P]).then_inc(taken, 1)
                dve.wait_ge(taken, 3 * WPP)
                st.mark(V.tensor_copy(S.rel_b[:], S.rel[:]))
                st.then(V.tensor_copy(tmp[:], S.src_m[:]))
                st.then(V.tensor_scalar(line_i[:, 0, :], tmp[:], 7, None, ALU.arith_shift_right))
                st.then(V.tensor_scalar(tmp[:], tmp[:], P - 1, None, ALU.bitwise_and))
                st.mark(V.tensor_copy(S.lo_b[:], tmp[:]))
                st.then(V.tensor_copy(S.hi_b[:], line_i[:, 0, :]))
                st.then(V.tensor_scalar(S.hi128_b[:], S.hi_b[:], float(P), None, ALU.mult))

            @block.tensor
            def _(pe):
                pe.wait_ge(counted, 1)
                nc.tensor.matmul(S.bank[0][:, 0:NB], S.ones[:], cnt[:], start=True, stop=True).then_inc(summed, 1)
                pe.wait_ge(lines, 1)
                for n in range(3 * WPP):
                    k, j = divmod(n, WPP)
                    if n >= 7:
                        pe.wait_ge(taken, n - 6)
                    nc.tensor.transpose(S.bank[1 + n % 7][:, 0:P], (ls, rel, bw)[k][:, j * P:(j + 1) * P],
                                        S.ident[:]).then_inc(turned, 1)



def made2(h):
    return 2 * RING + h + 1


def room2(h):
    return h + 1


def window_blocks(nc, S, engine, i):
    _, blocks = nc.values_load_multi_w_load_instructions(
        S.blk_row[0:1, bass.ds(i * BODY, BODY)], engines=(engine,), min_val=0, max_val=NB - 1,
        skip_runtime_bounds_check_because="the table holds counts of at most NB - 1 blocks")
    return blocks



def degrees(nc, S):
    ctx, sb, sem = scope(nc, "deg")
    half = BODY // 2
    with ctx:
        rows = sb("rows", [P, P, half], BF16)
        hot_lo = sb("hot_lo", [P, 2, P, half], BF16)
        hot_hi = sb("hot_hi", [P, 2, NB, half], BF16)
        node = sb("node", [P, NB])
        deg = sb("deg", [P, NB])
        root = sb("root", [P, NB])
        made, ready, used, spread = sem("made"), sem("ready"), sem("used"), sem("spread")
        total, dved, rooted = sem("total"), sem("dved"), sem("rooted")
        sums = S.bank[0][:, 0:NB]
        with nc.Block() as block:

            @block.gpsimd
            def _(pool):
                nc.gpsimd.iota(node[:], pattern=[[P, NB]], base=0, channel_multiplier=1,
                               allow_small_or_imprecise_dtypes=True).then_inc(made, 1)
                nc.gpsimd.memset(S.zero_b[:], 0.0).then_inc(made, 1)

            @block.vector
            def _(dve):
                V = nc.vector
                V.tensor_copy(rows[:], bc(S.row[:].unsqueeze(2), [P, P, half])).then_inc(spread, 1)
                dve.wait_ge(spread, 1)
                with dve.Fori(0, N_IT) as i:
                    for h in range(2):
                        w = i * BODY + h * half
                        dve.wait_ge(used, i * 2 + (h + 1))
                        for hot, of, n in ((hot_lo, S.lo_b, P), (hot_hi, S.hi_b, NB)):
                            V.tensor_tensor(hot[:, h], bc(of[:, bass.ds(w, half)].unsqueeze(1), [P, n, half]),
                                            rows[:, 0:n], ALU.is_equal).then_inc(ready, 1)
                dve.wait_ge(total, 1)
                st = Steps(dve, dved)
                st.then(V.tensor_scalar(node[:], node[:], float(N), None, ALU.is_ge))
                st.then(V.tensor_tensor(deg[:], sums, node[:], ALU.add))
                dve.wait_ge(rooted, 1)
                st.then(V.reciprocal(S.dinv[:], root[:]))

            @block.scalar
            def _(act):
                act.wait_ge(dved, 2)
                nc.scalar.activation(root[:], deg[:], ACT.Sqrt).then_inc(rooted, 1)

            @block.tensor
            def _(pe):
                pe.sem_inc(used, 2)
                pe.wait_ge(made, 2)
                nc.tensor.matmul(sums, S.zero_b[:], S.zero_b[:, 0:NB], start=True, stop=False)
                with pe.Fori(0, N_IT) as i:
                    for h in range(2):
                        pe.wait_ge(ready, i * 4 + 2 * (h + 1))
                        for k in range(half):
                            last = nc.tensor.matmul(sums, hot_lo[:, h, :, k], hot_hi[:, h, :, k], start=False, stop=False,
                                                    skip_group_check=True)
                        last.then_inc(used, 1)
                nc.tensor.matmul(sums, S.zero_b[:], S.zero_b[:, 0:NB], start=False,
                                 stop=True).then_inc(total, 1)


def load_nodes(nc, stage, x, into):
    ctx, sb, sem = scope(nc, stage)
    with ctx:
        cleared, loaded = sem("cleared"), sem("loaded")
        full = (NBLK - 1) * P
        with nc.Block() as block:

            @block.gpsimd
            def _(pool):
                nc.gpsimd.memset(into[:, (NBLK - 1) * D:NB * D], 0.0).then_inc(cleared, 1)

            @block.sync
            def _(sp):
                sp.dma_start(into[:, 0:(NBLK - 1) * D].rearrange("p (b d) -> p b d", d=D),
                             x[0:full, :].rearrange("(b p) d -> p b d", p=P)).then_inc(loaded, 16)
                sp.wait_ge(cleared, 1)
                sp.dma_start(into[0:TAIL, (NBLK - 1) * D:NBLK * D], x[full:N, :]).then_inc(loaded, 16)
                sp.wait_ge(loaded, 32)


def normalise(nc, S, stage, x, z, scale=None):
    ctx, sb, sem = scope(nc, stage)
    step = 5
    with ctx:
        stats = sb("stats", [P, NB, 6])
        mean = sb("mean", [P, NB])
        var = sb("var", [P, NB])
        rstd = sb("rstd", [P, NB])
        stated, dved, rooted, out = sem("stated"), sem("dved"), sem("rooted"), sem("out")
        flat = stats[:].rearrange("p b s -> p (b s)")
        with nc.Block() as block:

            @block.vector
            def _(dve):
                V = nc.vector
                st = Steps(dve, dved)
                with dve.Fori(0, NB // step) as i:
                    for k in range(step):
                        V.bn_stats(flat[:, bass.ds(i * (step * 6) + 6 * k, 6)],
                                   x[:, bass.ds(i * (step * D) + k * D, D)]).then_inc(stated, 1)
                dve.wait_ge(stated, NB)
                st.then(V.tensor_tensor(mean[:], stats[:, :, 1], stats[:, :, 4], ALU.add))
                st.then(V.tensor_tensor(var[:], stats[:, :, 1], stats[:, :, 4], ALU.subtract))
                st.then(V.tensor_tensor(var[:], var[:], var[:], ALU.mult))
                st.then(V.tensor_tensor(rstd[:], stats[:, :, 2], stats[:, :, 5], ALU.add))
                st.then(V.tensor_scalar(var[:], var[:], 0.25, EPS, ALU.mult, ALU.add))
                st.then(V.scalar_tensor_tensor(out=var[:], in0=rstd[:], scalar=1.0 / D, in1=var[:],
                                               op0=ALU.mult, op1=ALU.add))
                st.then(V.tensor_scalar(mean[:], mean[:], 0.5, None, ALU.mult))
                dve.wait_ge(rooted, 1)
                st.then(V.reciprocal(rstd[:], var[:]))
                if scale is not None:
                    st.then(V.tensor_tensor(rstd[:], rstd[:], scale[:], ALU.mult))
                with dve.Fori(0, NB // step) as i:
                    for k in range(step):
                        b = i * step + k
                        V.tensor_scalar(z[:, bass.ds(b * D, D)], x[:, bass.ds(b * D, D)], mean[:, bass.ds(b, 1)],
                                        rstd[:, bass.ds(b, 1)], ALU.subtract, ALU.mult).then_inc(out, 1)
                dve.wait_ge(out, NB)

            @block.scalar
            def _(act):
                act.wait_ge(dved, 6)
                nc.scalar.activation(var[:], var[:], ACT.Sqrt).then_inc(rooted, 1)



def gcn_scatter(nc, S, T, y):
    ctx, sb, sem = scope(nc, "gcn")
    with ctx:
        zero = sb("zero", [P, D])
        target = sb("target", [P, WL])
        spare = sb("spare", [P, 1])
        same = sb("same", [P, 2, GROUP * P], BF16)
        hot = sb("hot", [P, 2, GROUP * P], BF16)
        earlier = sb("earlier", [P, GROUP * P], BF16)
        n_earlier = sb("n_earlier", [P, GROUP])
        pick = sb("pick", [P, GROUP])
        idx = sb("idx", [P, SLOTS, GROUP], I32)
        spread = sb("spread", [P, 2, GROUP * P])
        msg = sb("msg", [P, SLOTS, GROUP, D])
        made, self_out, prep = sem("made"), sem("self_out"), sem("prep")
        src_out, same_made, hot_made = sem("src_out"), sem("same_made"), sem("hot_made")
        spread_out, spread_made = sem("spread_out"), sem("spread_made")
        msg_out, msg_made = sem("msg_out"), sem("msg_made")
        earlier_made, counted, picked, idx_made = sem("earlier_made"), sem("counted"), sem("picked"), sem("idx_made")
        landed, passed = sem("landed"), sem("passed")
        added = [sem(f"added{k}") for k in range(GROUP)]
        v4 = lambda t: t.rearrange("p (k e) -> p k e", k=GROUP)
        shape = [P, GROUP, P]
        with nc.Block() as block:

            @block.sync
            def _(sp):
                sp.dma_start(T.acc[0][0:N_PAD, :].rearrange("(b p) d -> p b d", p=P),
                             y[:].rearrange("p (b d) -> p b d", d=D)).then_inc(self_out, 16)
                sp.wait_ge(self_out, 16)

            @block.gpsimd
            def _(pool):
                nc.gpsimd.iota(spare[:], pattern=[[0, 1]], base=N_PAD, channel_multiplier=1,
                               allow_small_or_imprecise_dtypes=True).then_inc(made, 1)
                nc.gpsimd.memset(zero[:], 0.0).then_inc(made, 1)
                pool.wait_ge(made, 2)
                for k in range(GROUP):
                    first = NB if k == 0 else 0
                    pool.dma_start(T.acc[k][first * P:(NB + 1) * P, :].rearrange("(b p) d -> p b d", p=P),
                                   bc(zero[:, None, :], [P, NB + 1 - first, D])).then_inc(added[k], 16)
                pool.wait_ge(self_out, 16)
                pool.sem_inc(landed, SLOTS)
                with pool.Fori(0, N_IT) as i:
                    for s in range(SLOTS):
                        g = i * SLOTS + s
                        pool.wait_ge(idx_made, g + 1)
                        pool.wait_ge(msg_made, g * 2 + made2(1))
                        for k in range(GROUP):
                            pool.wait_ge(added[k], g * 16 + 16)
                            pool.sem_inc(landed if k == GROUP - 1 else passed, 1)
                            nc.gpsimd.indirect_dma_start(
                                out=T.acc[k], in_=msg[:, s, k], in_offset=None, compute_op=ALU.add,
                                out_offset=bass.IndirectOffsetOnAxis(ap=idx[:, s, k:k + 1].bitcast(U32), axis=0),
                            ).then_inc(added[k], 16)
                for k in range(GROUP):
                    pool.wait_ge(added[k], N_WIN // GROUP * 16 + 16)

            @block.vector
            def _(dve):
                V = nc.vector
                st = Steps(dve, prep)
                dve.sem_inc(same_made, RING)
                dve.wait_ge(made, 2)
                st.then(V.tensor_scalar(target[:], S.src_m[:], spare[:, 0:1], None, ALU.subtract))
                st.then(V.scalar_tensor_tensor(out=target[:], in0=S.src_m[:], scalar=0.0, in1=target[:],
                                               op0=ALU.is_ge, op1=ALU.mult))
                with dve.Fori(0, N_IT) as i:
                    for s in range(SLOTS):
                        q, g, w = s % 2, i * SLOTS + s, i * BODY + s * GROUP
                        dve.wait_ge(src_out, g + MADE)
                        dve.wait_ge(spread_out, g + ROOM)
                        V.tensor_tensor(v4(same[:, q]), v4(S.bank[q][:]),
                                        bc(S.src_m[:, bass.ds(w, GROUP)].unsqueeze(2), shape),
                                        ALU.is_equal).then_inc(same_made, 1)
                        V.tensor_tensor(v4(hot[:, q]), bc(S.rel_b[:, bass.ds(w, GROUP)].unsqueeze(2), shape),
                                        bc(S.row_b[:, None, :], shape), ALU.is_equal).then_inc(hot_made, 1)
                        dve.wait_ge(same_made, g + MADE)
                        V.tensor_tensor(v4(earlier[:]), v4(same[:, q]), bc(S.lower_b[:, None, :], shape),
                                        ALU.mult).then_inc(earlier_made, 1)
                        dve.wait_ge(earlier_made, g + 1)
                        V.tensor_reduce(n_earlier[:], v4(earlier[:]), AX.X, ALU.add).then_inc(counted, 1)
                        dve.wait_ge(counted, g + 1)
                        V.scalar_tensor_tensor(out=pick[:], in0=n_earlier[:], scalar=0.5,
                                               in1=target[:, bass.ds(w, GROUP)],
                                               op0=ALU.is_lt, op1=ALU.mult).then_inc(picked, 1)
                        dve.wait_ge(picked, g + 1)
                        dve.wait_ge(landed, g + 2)
                        V.tensor_scalar(idx[:, s], pick[:], spare[:, 0:1], None, ALU.add).then_inc(idx_made, 1)

            @block.scalar
            def _(act):
                act.sem_inc(spread_made, RING)
                act.sem_inc(msg_made, 2 * RING)
                with act.Fori(0, N_IT) as i:
                    for s in range(SLOTS):
                        q, g = s % 2, i * SLOTS + s
                        act.wait_ge(spread_out, g + MADE)
                        act.wait_ge(msg_out, g * 2 + room2(1))
                        nc.scalar.copy(spread[:, q], S.bank[2 + q][:]).then_inc(spread_made, 1)
                        act.wait_ge(landed, g + 2)
                        for h in range(2):
                            act.wait_ge(msg_out, g * 2 + made2(h))
                            nc.scalar.copy(msg[:, s, 2 * h:2 * h + 2].rearrange("p k d -> p (k d)"),
                                           S.bank[4 + 2 * q + h][:]).then_inc(msg_made, 1)

            @block.tensor
            def _(pe):
                def sources(g, q, w):
                    pe.wait_ge(same_made, g + ROOM)
                    pe.sem_inc(passed, 1)
                    for k in range(GROUP):
                        to = S.bank[q][:, k * P:(k + 1) * P]
                        nc.tensor.matmul(to, bc(S.lo_b[:, bass.ds(w + k, 1)], [P, P]), S.ident_b[:],
                                         start=True, stop=False)
                        last = nc.tensor.matmul(to, bc(S.hi128_b[:, bass.ds(w + k, 1)], [P, P]), S.ident_b[:],
                                                start=False, stop=True)
                    last.then_inc(src_out, 1)

                pe.sem_inc(src_out, RING)
                pe.sem_inc(spread_out, RING)
                pe.sem_inc(msg_out, 2 * RING)
                sources(0, 0, 0)
                with pe.Fori(0, N_IT) as i:
                    blocks = window_blocks(nc, S, ET.PE, i)
                    for s in range(SLOTS):
                        q, g, w = s % 2, i * SLOTS + s, i * BODY + s * GROUP
                        sources(g + 1, 1 - q, w + GROUP)
                        pe.wait_ge(hot_made, g + 1)
                        pe.wait_ge(same_made, g + MADE)
                        pe.wait_ge(spread_made, g + ROOM)
                        for k in range(GROUP):
                            e = slice(k * P, (k + 1) * P)
                            last = nc.tensor.matmul(S.bank[2 + q][:, e], hot[:, q, e], same[:, q, e],
                                                    start=True, stop=True)
                        last.then_inc(spread_out, 1)
                        pe.wait_ge(spread_made, g + MADE)
                        for h in range(2):
                            pe.wait_ge(msg_made, g * 2 + room2(h))
                            for k in (2 * h, 2 * h + 1):
                                last = nc.tensor.matmul(
                                    S.bank[4 + 2 * q + h][:, (k % 2) * D:(k % 2 + 1) * D],
                                    spread[:, q, k * P:(k + 1) * P],
                                    y[:, bass.ds(blocks[s * GROUP + k] * D, D)], start=True, stop=True)
                            last.then_inc(msg_out, 1)


def transposed_weight(nc, S, stage, w, into):
    ctx, sb, sem = scope(nc, stage)
    with ctx:
        rows = sb("rows", [P, 2, D])
        loaded, turned, taken = sem("loaded"), sem("turned"), sem("taken")
        with nc.Block() as block:

            @block.sync
            def _(sp):
                sp.dma_start(rows[:], w.rearrange("(o p) i -> p o i", p=P)).then_inc(loaded, 16)

            @block.tensor
            def _(pe):
                pe.wait_ge(loaded, 16)
                for c in range(2):
                    for o in range(2):
                        last = nc.tensor.transpose(S.bank[c][:, o * P:(o + 1) * P], rows[:, o, c * P:(c + 1) * P],
                                                   S.ident[:])
                last.then_inc(turned, 1)

            @block.vector
            def _(dve):
                dve.wait_ge(turned, 1)
                for c in range(2):
                    nc.vector.tensor_copy(into[:, c, 0:D], S.bank[c][:, 0:D]).then_inc(taken, 1)
                dve.wait_ge(taken, 2)


def project(nc, S, stage, weight, cols, feed, post, posts):
    ctx, sb, sem = scope(nc, stage)
    with ctx:
        rows = [sb(f"rows{q}", [P, D]) for q in range(2)]
        turned = [sb(f"turned{q}", [P, 2, P]) for q in range(2)]
        fed, turn_out, turn_made = sem("fed"), sem("turn_out"), sem("turn_made")
        prod_out, done, passed = sem("prod_out"), sem("done"), sem("passed")
        local = posts(sb, sem)
        with nc.Block() as block:

            @block.vector
            def _(dve):
                def feed_block(b, q):
                    dve.wait_ge(turn_out, b + ROOM)
                    feed(nc.vector, b, rows[q]).then_inc(fed, 1)

                def post_block(b, q):
                    dve.wait_ge(prod_out, b + MADE)
                    post(nc.vector, dve, b, S.bank[2 + q][:, 0:cols], q, local).then_inc(done, 1)

                dve.sem_inc(done, RING)
                feed_block(0, 0)
                feed_block(1, 1)
                with dve.Fori(0, NB // 2 - 1) as i:
                    for q in range(2):
                        feed_block(i * 2 + (q + 2), q)
                        post_block(i * 2 + q, q)
                for q in range(2):
                    post_block(NB - 2 + q, q)
                dve.wait_ge(done, NB + RING)

            @block.scalar
            def _(act):
                act.sem_inc(turn_made, RING)
                with act.Fori(0, NB // 2) as i:
                    for q in range(2):
                        b = i * 2 + q
                        act.wait_ge(turn_out, b + MADE)
                        act.wait_ge(prod_out, b + ROOM)
                        nc.scalar.copy(turned[q][:].rearrange("p c n -> p (c n)"),
                                       S.bank[q][:, 0:2 * P]).then_inc(turn_made, 1)

            @block.tensor
            def _(pe):
                def turn(b, q):
                    pe.wait_ge(fed, b + 1)
                    pe.wait_ge(turn_made, b + ROOM)
                    for c in range(2):
                        last = nc.tensor.transpose(S.bank[q][:, c * P:(c + 1) * P], rows[q][:, c * P:(c + 1) * P],
                                                   S.ident[:])
                    last.then_inc(turn_out, 1)

                def multiply(b, q):
                    pe.wait_ge(turn_made, b + MADE)
                    pe.wait_ge(done, b + ROOM)
                    for c in range(2):
                        last = nc.tensor.matmul(S.bank[2 + q][:, 0:cols], turned[q][:, c, :], weight[:, c, 0:cols],
                                                start=(c == 0), stop=(c == 1))
                    last.then_inc(prod_out, 1)

                pe.sem_inc(turn_out, RING)
                pe.sem_inc(prod_out, RING)
                turn(0, 0)
                with pe.Fori(0, NB // 2 - 1) as i:
                    for q in range(2):
                        turn(i * 2 + (q + 1), 1 - q)
                        multiply(i * 2 + q, q)
                turn(NB - 1, 1)
                multiply(NB - 2, 0)
                multiply(NB - 1, 1)


def gcn_out(nc, S, T, A, x, z):
    ctx, sb, sem = scope(nc, "gcn_out")
    with ctx:
        weight = sb("weight", [P, 2, D])
        bias = sb("bias", [P, D])
        loaded, summed = sem("loaded"), sem("summed")
        transposed_weight(nc, S, "gcn_w", A["L0_gnn_W"], weight)
        with nc.Block() as block:

            @block.sync
            def _(sp):
                sp.dma_start(bias[:], bc(A["L0_gnn_b"].rearrange("(a d) -> a d", a=1), [P, D])).then_inc(loaded, 16)
                sp.wait_ge(loaded, 16)

            @block.gpsimd
            def _(pool):
                view = z[:].rearrange("p (b d) -> p b d", d=D)
                for k in range(GROUP):
                    how = {"accum_op": ALU.add} if k else {}
                    pool.dma_start(view, T.acc[k][0:N_PAD, :].rearrange("(b p) d -> p b d", p=P),
                                   **how).then_inc(summed, 16)
                    pool.wait_ge(summed, 16 * (k + 1))

        def feed(V, b, rows):
            return V.tensor_scalar(rows[:], z[:, bass.ds(b * D, D)], S.dinv[:, bass.ds(b, 1)], None, ALU.mult)

        def posts(sb, sem):
            return [sb(f"t{q}", [P, D]) for q in range(2)], sem("biased")

        def post(V, dve, b, out, q, local):
            t, biased = local
            V.tensor_tensor(t[q][:], out, bias[:], ALU.add).then_inc(biased, 1)
            dve.wait_ge(biased, b + 1)
            return V.scalar_tensor_tensor(out=x[:, bass.ds(b * D, D)], in0=t[q][:], scalar=0.0,
                                          in1=x[:, bass.ds(b * D, D)], op0=ALU.max, op1=ALU.add)

        project(nc, S, "gcn_proj", weight, D, feed, post, posts)

N_EXP, TOP_K, F = 8, 2, 512
FC = F // P
CAPACITY = -(-(N * 5) // (4 * N_EXP))


def route(nc, S, A, z, top_w, top_i):
    ctx, sb, sem = scope(nc, "route")
    with ctx:
        in_tail = sb("in_tail", [P, P])
        wr = sb("wr", [P, 2, N_EXP])
        br = sb("br", [P, N_EXP])
        mean = sb("mean", [P, D])
        mean_t = sb("mean_t", [P, 2, P])
        r, e, load = (sb(n, [P, N_EXP]) for n in ("r", "e", "load"))
        one = sb("one", [P, 1])
        best = sb("best", [P, 8])
        loaded, made, dved, expd = sem("loaded"), sem("made"), sem("dved"), sem("expd")
        summed, turned, multiplied, meaned, mean_turned = (
            sem(n) for n in ("summed", "turned", "multiplied", "meaned", "mean_turned"))
        with nc.Block() as block:

            @block.sync
            def _(sp):
                sp.dma_start(wr[:], A["L0_ffn_Wr"].rearrange("(c p) e -> p c e", p=P)).then_inc(loaded, 16)
                sp.dma_start(br[:], bc(A["L0_ffn_br"].rearrange("(a e) -> a e", a=1), [P, N_EXP])).then_inc(loaded, 16)

            @block.gpsimd
            def _(pool):
                nc.gpsimd.memset(in_tail[:], 1.0).then_inc(made, 1)
                pool.wait_ge(made, 1)
                nc.gpsimd.affine_select(out=in_tail[:], in_=in_tail[:], compare_op=ALU.is_gt, fill=0.0,
                                        base=TAIL, pattern=[[0, P]], channel_multiplier=-1).then_inc(made, 1)

            @block.tensor
            def _(pe):
                total = S.bank[0][:, 0:D]
                nc.tensor.matmul(total, S.ones[:], z[:, 0:D], start=True, stop=False)
                with pe.Fori(1, NBLK - 1) as b:
                    nc.tensor.matmul(total, S.ones[:], z[:, bass.ds(b * D, D)], start=False, stop=False,
                                     skip_group_check=True)
                pe.wait_ge(made, 2)
                nc.tensor.matmul(total, in_tail[:], z[:, (NBLK - 1) * D:NBLK * D], start=False,
                                 stop=True).then_inc(summed, 1)
                pe.wait_ge(meaned, 1)
                for c in range(2):
                    last = nc.tensor.transpose(S.bank[1][:, c * P:(c + 1) * P], mean[:, c * P:(c + 1) * P], S.ident[:])
                last.then_inc(turned, 1)
                pe.wait_ge(mean_turned, 1)
                pe.wait_ge(loaded, 32)
                for c in range(2):
                    last = nc.tensor.matmul(S.bank[2][:, 0:N_EXP], mean_t[:, c, :], wr[:, c, :],
                                            start=(c == 0), stop=(c == 1))
                last.then_inc(multiplied, 1)

            @block.scalar
            def _(act):
                for k in range(2):
                    act.wait_ge(made, 3 + k)
                    nc.scalar.activation(e[:], r[:], ACT.Exp).then_inc(expd, 1)
                act.wait_ge(made, 5)
                nc.scalar.activation(top_w[:, 1:2], top_w[:, 1:2], ACT.Exp).then_inc(expd, 1)

            @block.vector
            def _(dve):
                V = nc.vector
                st = Steps(dve, dved)

                def softmax(k):
                    st.then(V.tensor_reduce(one[:], r[:], AX.X, ALU.max))
                    V.tensor_scalar(r[:], r[:], one[:, 0:1], None, ALU.subtract).then_inc(made, 1)
                    dve.wait_ge(expd, k + 1)
                    st.then(V.tensor_reduce(one[:], e[:], AX.X, ALU.add))
                    st.then(V.reciprocal(one[:], one[:]))
                    st.then(V.tensor_scalar(r[:], e[:], one[:, 0:1], None, ALU.mult))

                dve.wait_ge(summed, 1)
                V.tensor_scalar(mean[:], S.bank[0][:, 0:D], 1.0 / N, None, ALU.mult).then_inc(meaned, 1)
                dve.wait_ge(turned, 1)
                V.tensor_copy(mean_t[:].rearrange("p c n -> p (c n)"), S.bank[1][:, 0:D]).then_inc(mean_turned, 1)
                dve.wait_ge(multiplied, 1)
                dve.wait_ge(loaded, 32)
                dve.wait_ge(made, 2)
                st.then(V.tensor_tensor(r[:], S.bank[2][:, 0:N_EXP], br[:], ALU.add))
                softmax(0)
                st.then(V.tensor_scalar(load[:], r[:], float(N), None, ALU.mult))
                st.then(V.reciprocal(load[:], load[:]))
                st.then(V.tensor_scalar(load[:], load[:], float(CAPACITY), 1.0, ALU.mult, ALU.min))
                st.then(V.tensor_tensor(r[:], r[:], load[:], ALU.mult))
                softmax(1)
                st.then(V.max(best[:], r[:]))
                st.then(V.max_index(top_i[:], best[:], r[:]))
                V.tensor_tensor(top_w[:, 1:2], best[:, 1:2], best[:, 0:1], ALU.subtract).then_inc(made, 1)
                dve.wait_ge(expd, 3)
                st.then(V.tensor_scalar(one[:], top_w[:, 1:2], 1.0, None, ALU.add))
                st.then(V.reciprocal(top_w[:, 0:1], one[:]))
                st.then(V.tensor_tensor(top_w[:, 1:2], top_w[:, 1:2], top_w[:, 0:1], ALU.mult))


def experts(nc, S, T, A, x, z):
    ctx, sb, sem = scope(nc, "ffn")
    with ctx:
        top_w = sb("top_w", [P, TOP_K])
        top_i = sb("top_i", [P, 8], U32)
        w1 = sb("w1", [P, TOP_K, 2, F])
        w2 = sb("w2", [P, TOP_K, FC, D])
        b1 = sb("b1", [P, TOP_K, FC])
        b2 = sb("b2", [1, TOP_K, D])
        route(nc, S, A, z, top_w, top_i)
        loaded, scaled, b2_made = sem("loaded"), sem("scaled"), sem("b2_made")
        with nc.Block() as block:

            @block.sync
            def _(sp):
                for j in range(TOP_K):
                    e = sp.value_load(top_i[0:1, j:j + 1].bitcast(I32), min_val=0, max_val=N_EXP - 1)
                    pick = lambda name: A[name][bass.ds(e, 1)]
                    for to, of in (
                        (w1[:, j], pick("L0_ffn_W1").rearrange("a (c p) f -> p (a c) f", p=P)),
                        (w2[:, j], pick("L0_ffn_W2").rearrange("a (c p) d -> p (a c) d", p=P)),
                        (b1[:, j], pick("L0_ffn_b1").rearrange("a (c p) -> p (a c)", p=P)),
                        (b2[0:1, j], pick("L0_ffn_b2")),
                    ):
                        sp.dma_start(to, of, allow_slow_non_contiguous=True).then_inc(loaded, 16)
                sp.wait_ge(loaded, 16 * 4 * TOP_K)

            @block.vector
            def _(dve):
                V = nc.vector
                dve.wait_ge(loaded, 16 * 4 * TOP_K)
                for j in range(TOP_K):
                    V.tensor_scalar(w2[:, j], w2[:, j], top_w[:, j:j + 1], None, ALU.mult).then_inc(scaled, 1)
                    V.tensor_scalar(b2[0:1, j], b2[0:1, j], top_w[0:1, j:j + 1], None, ALU.mult).then_inc(scaled, 1)
                dve.wait_ge(scaled, 2 * TOP_K)
                V.tensor_tensor(b2[0:1, 0], b2[0:1, 0], b2[0:1, 1], ALU.add).then_inc(b2_made, 1)
                dve.wait_ge(b2_made, 1)

        H = TOP_K * FC
        HB = H // 2
        rows = [sb(f"rows{q}", [P, 2, D]) for q in range(2)]
        turned = [sb(f"turned{q}", [P, 2, 2 * P]) for q in range(2)]
        hidden = [sb(f"hidden{q}", [P, H, 2 * P]) for q in range(2)]
        fed, turn_out, turn_made = sem("fed"), sem("turn_out"), sem("turn_made")
        hidden_out, hidden_made = sem("hidden_out"), sem("hidden_made")
        prod_out, done = sem("prod_out"), sem("done")
        PAIRS = NB // 2
        turn_bank, hidden_bank, prod_bank = S.bank[0], S.bank[1:5], S.bank[5:7]

        def pairs(engine, body):
            with engine.Fori(0, PAIRS // 2) as i:
                body(i * 2, 0)
                body(i * 2 + 1, 1)
            body(PAIRS - 1, 0)

        with nc.Block() as block:

            @block.vector
            def _(dve):
                V = nc.vector

                def feed(u, q):
                    dve.wait_ge(turn_out, u + ROOM)
                    V.tensor_copy(rows[q][:].rearrange("p k d -> p (k d)"),
                                  z[:, bass.ds(u * (2 * D), 2 * D)]).then_inc(fed, 1)

                def post(u, q):
                    for k in range(2):
                        dve.wait_ge(prod_out, u * 2 + made2(k))
                        at = z[:, bass.ds(u * (2 * D) + k * D, D)]
                        V.tensor_tensor(at, prod_bank[k][:, 0:D], at, ALU.add).then_inc(done, 1)

                dve.sem_inc(done, 2)
                feed(0, 0)
                feed(1, 1)
                with dve.Fori(0, PAIRS // 2 - 1) as i:
                    for q in range(2):
                        feed(i * 2 + (q + 2), q)
                        post(i * 2 + q, q)
                feed(PAIRS - 1, 0)
                post(PAIRS - 3, 0)
                post(PAIRS - 2, 1)
                post(PAIRS - 1, 0)
                dve.wait_ge(done, NB + 2)

            @block.scalar
            def _(act):
                def body(u, q):
                    act.wait_ge(turn_out, u + MADE)
                    act.wait_ge(hidden_out, u * HB + HB)
                    nc.scalar.copy(turned[q][:].rearrange("p c n -> p (c n)"), turn_bank[:]).then_inc(turn_made, 1)
                    act.wait_ge(prod_out, u * 2 + room2(1))
                    for n in range(HB):
                        act.wait_ge(hidden_out, u * HB + (n + 1 + 2 * HB))
                        for h in (2 * n, 2 * n + 1):
                            last = nc.scalar.activation(
                                hidden[q][:, h, :], hidden_bank[n][:, h % 2 * D:(h % 2 + 1) * D], ACT.Gelu,
                                bias=b1[:, h // FC, h % FC:h % FC + 1])
                        last.then_inc(hidden_made, 1)

                act.sem_inc(hidden_made, HB)
                pairs(act, body)

            @block.tensor
            def _(pe):
                def turn(u, q):
                    pe.wait_ge(fed, u + 1)
                    for c in range(2):
                        for k in range(2):
                            last = nc.tensor.transpose(turn_bank[:, (2 * c + k) * P:(2 * c + k + 1) * P],
                                                       rows[q][:, k, c * P:(c + 1) * P], S.ident[:])
                    last.then_inc(turn_out, 1)

                def hide(u, q):
                    pe.wait_ge(turn_made, u + 1)
                    for h in range(H):
                        j, f = divmod(h, FC)
                        if h % 2 == 0:
                            pe.wait_ge(hidden_made, u * HB + (h // 2 + 1))
                        for c in range(2):
                            last = nc.tensor.matmul(hidden_bank[h // 2][:, h % 2 * D:(h % 2 + 1) * D],
                                                    w1[:, j, c, f * P:(f + 1) * P], turned[q][:, c, :],
                                                    start=(c == 0), stop=(c == 1))
                        if h % 2:
                            last.then_inc(hidden_out, 1)

                def combine(u, q):
                    pe.wait_ge(hidden_made, u * HB + 2 * HB)
                    for k in range(2):
                        pe.wait_ge(done, u * 2 + (k + 1))
                        to = prod_bank[k][:, 0:D]
                        nc.tensor.matmul(to, S.ones[0:1, :], b2[0:1, 0, :], start=True, stop=False)
                        for h in range(H):
                            last = nc.tensor.matmul(to, hidden[q][:, h, k * P:(k + 1) * P], w2[:, h // FC, h % FC, :],
                                                    start=False, stop=(h == H - 1))
                        last.then_inc(prod_out, 1)

                pe.sem_inc(turn_out, RING)
                pe.sem_inc(hidden_out, 2 * HB)
                pe.sem_inc(prod_out, 2 * RING)
                turn(0, 0)
                hide(0, 0)
                turn(1, 1)
                with pe.Fori(0, PAIRS // 2 - 1) as i:
                    for q in range(2):
                        hide(i * 2 + (q + 1), 1 - q)
                        turn(i * 2 + (q + 2), q)
                        combine(i * 2 + q, q)
                hide(PAIRS - 2, 1)
                turn(PAIRS - 1, 0)
                combine(PAIRS - 3, 0)
                hide(PAIRS - 1, 0)
                combine(PAIRS - 2, 1)
                combine(PAIRS - 1, 0)

        normalise(nc, S, "ffn_ln", z, z)
        gamma, beta = sb("gamma", [P, D]), sb("beta", [P, D])
        fetched, dved = sem("fetched"), sem("dved")
        with nc.Block() as block:

            @block.sync
            def _(sp):
                for to, name in ((gamma, "L0_ffn_gamma"), (beta, "L0_ffn_beta")):
                    sp.dma_start(to[:], bc(A[name].rearrange("(a d) -> a d", a=1), [P, D])).then_inc(fetched, 16)

            @block.vector
            def _(dve):
                V = nc.vector
                st = Steps(dve, dved)
                view = lambda t: t[:].rearrange("p (b d) -> p b d", d=D)
                dve.wait_ge(fetched, 32)
                st.mark(V.tensor_tensor(view(x), view(x), bc(beta[:, None, :], [P, NB, D]), ALU.add))
                st.then(V.tensor_tensor(view(z), view(z), bc(gamma[:, None, :], [P, NB, D]), ALU.mult))
                st.then(V.tensor_tensor(x[:], x[:], z[:], ALU.add))

class Masks:
    pass


def segment_masks(nc, S, M):
    ctx, sb, sem = scope(nc, "masks")
    last = LINE - 1
    with ctx:
        ends = sb("ends", [P, 4, HEADS])
        rows = sb("rows", [HEADS, 4, P])
        link = sb("link", [HEADS, 2, P])
        zero = sb("zero", [P, LINE])
        run = sb("run", [P, LINE])
        cols = sb("cols", [P, 2, HEADS])
        dved, ended, turned, linked, cols_out, runs, runs_out = (
            sem(n) for n in ("dved", "ended", "turned", "linked", "cols_out", "runs", "runs_out"))
        with nc.Block() as block:

            @block.tensor
            def _(pe):
                pe.wait_ge(ended, 2)
                for k in range(2):
                    last_i = nc.tensor.transpose(S.bank[0][0:HEADS, k * P:(k + 1) * P], ends[:, k], S.ident[:])
                last_i.then_inc(turned, 1)
                pe.wait_ge(linked, 2)
                for k in range(2):
                    last_i = nc.tensor.transpose(S.bank[1][:, k * HEADS:(k + 1) * HEADS], link[:, k],
                                                 S.ident[0:HEADS, 0:HEADS])
                last_i.then_inc(cols_out, 1)
                pe.wait_ge(runs, 2)
                for k in range(2):
                    last_i = nc.tensor.transpose(S.bank[2][0:HEADS, k * P:(k + 1) * P], ends[:, 2 + k], S.ident[:])
                last_i.then_inc(runs_out, 1)

            @block.vector
            def _(dve):
                V = nc.vector
                st = Steps(dve, dved)
                V.tensor_copy(ends[:, 0], bc(S.key[:, 0:1], [P, HEADS])).then_inc(ended, 1)
                V.tensor_copy(ends[:, 1], bc(S.key[:, last:], [P, HEADS])).then_inc(ended, 1)
                st.mark(V.memset(zero[:], 0.0))
                st.then(V.memset(link[:], 0.0))
                dve.wait_ge(turned, 1)
                st.then(V.tensor_copy(rows[:, 0:2].rearrange("h k p -> h (k p)"), S.bank[0][0:HEADS, 0:2 * P]))
                V.tensor_tensor(link[:, 0, 1:], rows[:, 0, 1:], rows[:, 1, 0:P - 1], ALU.is_equal).then_inc(linked, 1)
                V.tensor_tensor(link[:, 1, 0:P - 1], rows[:, 0, 1:], rows[:, 1, 0:P - 1],
                                ALU.is_equal).then_inc(linked, 1)
                dve.wait_ge(cols_out, 1)
                st.then(V.tensor_copy(cols[:].rearrange("p k h -> p (k h)"), S.bank[1][:, 0:2 * HEADS]))
                st.mark(V.tensor_tensor(M.keep_f[:, 1:], S.key[:, 1:], S.key[:, 0:last], ALU.is_equal))
                st.mark(V.tensor_tensor(M.keep_b[:, 0:last], S.key[:, 1:], S.key[:, 0:last], ALU.is_equal))
                st.mark(V.tensor_copy(M.keep_f[:, 0:1], cols[:, 0, 0:1]))
                st.then(V.tensor_copy(M.keep_b[:, last:], cols[:, 1, 0:1]))
                st.then(V.tensor_tensor_scan(M.open_f[:], M.keep_f[:], zero[:], 1.0, ALU.mult, ALU.add))
                st.then(V.tensor_tensor_scan(M.open_b[:, ::-1], M.keep_b[:, ::-1], zero[:], 1.0, ALU.mult, ALU.add))
                V.tensor_copy(ends[:, 2], bc(M.open_f[:, last:], [P, HEADS])).then_inc(runs, 1)
                V.tensor_copy(ends[:, 3], bc(M.open_b[:, 0:1], [P, HEADS])).then_inc(runs, 1)
                st.mark(V.memset(M.keep_f[:, 0:1], 0.0))
                st.mark(V.memset(M.keep_b[:, last:], 0.0))
                dve.wait_ge(runs, 2)
                dve.wait_ge(runs_out, 1)
                st.mark(V.memset(M.chain[:], 0.0))
                st.mark(V.tensor_copy(M.join[:], link[:]))
                st.then(V.tensor_copy(rows[:, 2:4].rearrange("h k p -> h (k p)"), S.bank[2][0:HEADS, 0:2 * P]))
                st.mark(V.tensor_tensor(M.chain[:, 0, 1:], link[:, 0, 1:], rows[:, 2, 0:P - 1], ALU.mult))
                st.then(V.tensor_tensor(M.chain[:, 1, 0:P - 1], link[:, 1, 0:P - 1], rows[:, 3, 1:], ALU.mult))
                for t in (M.keep_f, M.keep_b, M.open_f, M.open_b, M.chain, M.join):
                    st.mark(V.tensor_scalar(t[:], t[:], -1.0, BIG, ALU.add, ALU.mult))
                st.wait()


WROW = D + 2 * HEADS


def gat_tables(nc, S, T, A, layer, z, table):
    ctx, sb, sem = scope(nc, f"gat_t{layer}")
    with ctx:
        weight = sb("weight", [P, 2, WROW])
        attn = sb("attn", [P, 2, D])
        prod = sb("prod", [P, 2, 2, D])
        loaded, multiplied, reduced, stored = sem("loaded"), sem("multiplied"), sem("reduced"), sem("stored")
        with nc.Block() as block:

            @block.sync
            def _(sp):
                sp.dma_start(weight[:, :, 0:D],
                             A[f"L1_gnn_W{layer}"].rearrange("(c p) n -> p c n", p=P)).then_inc(loaded, 16)
                for k, side in enumerate("lr"):
                    row = A[f"L1_gnn_a{side}{layer}"].rearrange("h d -> (h d)").rearrange("(a n) -> a n", a=1)
                    sp.dma_start(attn[:, k], bc(row, [P, D])).then_inc(loaded, 16)

            @block.vector
            def _(dve):
                dve.wait_ge(loaded, 48)
                for k in range(2):
                    nc.vector.tensor_tensor(prod[:, k], weight[:, :, 0:D], bc(attn[:, k:k + 1, :], [P, 2, D]),
                                            ALU.mult).then_inc(multiplied, 1)
                dve.wait_ge(multiplied, 2)
                for k in range(2):
                    nc.vector.tensor_reduce(weight[:, :, D + k * HEADS:D + (k + 1) * HEADS],
                                            prod[:, k].rearrange("p c (h d) -> p c h d", h=HEADS),
                                            AX.X, ALU.add).then_inc(reduced, 1)
                dve.wait_ge(reduced, 2)

        def feed(V, b, rows):
            return V.tensor_copy(rows[:], z[:, bass.ds(b * D, D)])

        def post(V, dve, b, out, q, local):
            return V.tensor_copy(table[:, bass.ds(b * WROW, WROW)], out)

        project(nc, S, f"gat_p{layer}", weight, WROW, feed, post, lambda sb, sem: None)
        view = table[:].rearrange("p (b n) -> p b n", n=WROW)
        with nc.Block() as block:

            @block.sync
            def _(sp):
                for to, c in ((T.feat, slice(0, D)), (T.el, slice(D, D + HEADS))):
                    sp.dma_start(to.rearrange("(b p) n -> p b n", p=P), view[:, :, c]).then_inc(stored, 16)
                sp.wait_ge(stored, 32)


LOOKED = 2
GATHERED = GROUP - LOOKED


def gat_scores(nc, S, T, layer, table, score):
    ctx, sb, sem = scope(nc, f"gat_s{layer}")
    n_idx, n_looked, parts = GROUP * HEADS, LOOKED * HEADS, 3
    with ctx:
        parted = sb("parted", [P, parts, NB, 2 * HEADS], BF16)
        rest = sb("rest", [P, NB, 2 * HEADS])
        el_parts = sb("el_parts", [P, parts, HEADS, NBLK], BF16)
        er_parts = sb("er_parts", [P, NB, HEADS, parts], BF16)
        idx = sb("idx", [P, SLOTS, GATHERED], I32)
        el = sb("el", [P, SLOTS, n_idx])
        er = sb("er", [P, 2, n_idx])
        far = sb("far", [P, LOOKED * P], BF16)
        hot_lo = sb("hot_lo", [P, 2, LOOKED * P], BF16)
        hot_hi = sb("hot_hi", [P, 2, LOOKED, NBLK], BF16)
        hot_t = sb("hot_t", [P, 2, GROUP * P], BF16)
        rows = sb("rows", [P, LOOKED, HEADS, NBLK])
        cleared, idx_made, passed, split = sem("cleared"), sem("idx_made"), sem("passed"), sem("split")
        rel_out, lo_out, far_made, lo_made = sem("rel_out"), sem("lo_out"), sem("far_made"), sem("lo_made")
        hot_made, hi_made, er_out, rows_out = sem("hot_made"), sem("hi_made"), sem("er_out"), sem("rows_out")
        masked, er_made, el_made, scored = sem("masked"), sem("er_made"), sem("el_made"), sem("scored")
        got = [sem(f"got{s}") for s in range(SLOTS)]
        with nc.Block() as block:

            @block.gpsimd
            def _(pool):
                nc.gpsimd.memset(score[:, N_WIN * HEADS:], 0.0).then_inc(cleared, 1)
                with pool.Fori(0, N_IT) as i:
                    for s in range(SLOTS):
                        pool.wait_ge(idx_made, i * SLOTS + (s + 1))
                        pool.sem_inc(passed, 1)
                        for k in range(GATHERED):
                            nc.gpsimd.indirect_dma_start(
                                out=el[:, s, k * HEADS:(k + 1) * HEADS], out_offset=None, in_=T.el,
                                in_offset=bass.IndirectOffsetOnAxis(ap=idx[:, s, k:k + 1].bitcast(U32), axis=0),
                            ).then_inc(got[s], 16)
                for s in range(SLOTS):
                    pool.wait_ge(got[s], N_IT * 16 * GATHERED)

            @block.scalar
            def _(act):
                def indices(g, s, w):
                    act.wait_ge(scored, g + 1)
                    act.sem_inc(passed, 1)
                    nc.scalar.copy(idx[:, s], S.src_i[:, bass.ds(w, GATHERED)]).then_inc(idx_made, 1)

                act.sem_inc(lo_made, RING)
                act.sem_inc(far_made, RING)
                indices(0, 0, 0)
                indices(1, 1, GROUP)
                with act.Fori(0, N_IT) as i:
                    for s in range(SLOTS):
                        q, g = s % 2, i * SLOTS + s
                        indices(g + 2, (s + 2) % SLOTS, i * BODY + (s + 2) * GROUP)
                        act.wait_ge(lo_out, g + MADE)
                        act.wait_ge(lo_made, g + RING)
                        nc.scalar.activation(far[:], S.bank[2 + q][:, 0:LOOKED * P], ACT.Abs,
                                             bias=S.minus_col[:, 0:1]).then_inc(far_made, 1)
                        act.wait_ge(far_made, g + MADE)
                        act.wait_ge(rows_out, g + ROOM)
                        nc.scalar.activation(hot_lo[:, q], far[:], ACT.Relu, bias=1.0,
                                             scale=-1.0).then_inc(lo_made, 1)

            @block.vector
            def _(dve):
                V = nc.vector
                st = Steps(dve, split)
                st.then(V.tensor_copy(rest[:], table[:].rearrange("p (b n) -> p b n", n=WROW)[:, :, D:]))
                for n in range(parts):
                    st.then(V.tensor_copy(parted[:, n], rest[:]))
                    if n < parts - 1:
                        st.then(V.tensor_tensor(rest[:], rest[:], parted[:, n], ALU.subtract))
                for n in range(parts):
                    by_head = parted[:, n].rearrange("p b h -> p h b")
                    st.mark(V.tensor_copy(el_parts[:, n], by_head[:, 0:HEADS, 0:NBLK]))
                    st.mark(V.tensor_copy(er_parts[:, :, :, n], parted[:, n, :, HEADS:]))
                st.wait()
                dve.sem_inc(hot_made, RING)
                dve.sem_inc(scored, SLOTS)

                def hot(g, q):
                    dve.wait_ge(rel_out, g + MADE)
                    dve.wait_ge(er_out, g + ROOM)
                    V.tensor_scalar(hot_t[:, q], S.bank[q][:], S.col[:, 0:1], None, ALU.is_equal).then_inc(hot_made, 1)

                def hot_his(q, w):
                    shape = [P, LOOKED, NBLK]
                    V.tensor_tensor(hot_hi[:, q], bc(S.hi_b[:, bass.ds(w + GATHERED, LOOKED)].unsqueeze(2), shape),
                                    bc(S.row_b[:, None, 0:NBLK], shape), ALU.is_equal).then_inc(hi_made, 1)

                hot(0, 0)
                hot_his(0, 0)
                with dve.Fori(0, N_IT) as i:
                    for s in range(SLOTS):
                        q, g = s % 2, i * SLOTS + s
                        hot(g + 1, 1 - q)
                        dve.wait_ge(hi_made, g + 1)
                        dve.wait_ge(rows_out, g + MADE)
                        V.tensor_tensor(rows[:], S.bank[4 + q][:, 0:n_looked * NBLK].rearrange(
                            "p (k h b) -> p k h b", k=LOOKED, h=HEADS),
                            bc(hot_hi[:, q].unsqueeze(2), [P, LOOKED, HEADS, NBLK]), ALU.mult).then_inc(masked, 1)
                        dve.wait_ge(er_out, g + MADE)
                        V.tensor_reduce(er[:, q], S.bank[6 + q][:, 0:n_idx * parts].rearrange(
                            "p (n t) -> p n t", t=parts), AX.X, ALU.add).then_inc(er_made, 1)
                        dve.wait_ge(masked, g + 1)
                        V.tensor_reduce(el[:, s, GATHERED * HEADS:], rows[:].rearrange("p k h b -> p (k h) b"),
                                        AX.X, ALU.add).then_inc(el_made, 1)
                        hot_his(1 - q, i * BODY + (s + 1) * GROUP)
                        dve.wait_ge(el_made, g + 1)
                        dve.wait_ge(er_made, g + 1)
                        dve.wait_ge(got[s], i * (16 * GATHERED) + 16 * GATHERED)
                        V.tensor_tensor(score[:, bass.ds(i * (BODY * HEADS) + s * n_idx, n_idx)],
                                        er[:, q], el[:, s], ALU.add).then_inc(scored, 1)
                dve.wait_ge(cleared, 1)
                dve.wait_ge(hot_made, N_IT * SLOTS + MADE)
                dve.wait_ge(hi_made, N_IT * SLOTS + 1)
                dve.wait_ge(scored, N_IT * SLOTS + SLOTS)

            @block.tensor
            def _(pe):
                pe.sem_inc(rel_out, RING)
                pe.sem_inc(lo_out, RING)
                pe.sem_inc(er_out, RING)
                pe.sem_inc(rows_out, RING)

                def spread(g, q, w):
                    pe.wait_ge(hot_made, g + ROOM)
                    pe.wait_ge(far_made, g + ROOM)
                    pe.sem_inc(passed, 1)
                    for bank, of, first, out in ((S.bank[q], S.rel_b, 0, rel_out),
                                                 (S.bank[2 + q], S.lo_b, GATHERED, lo_out)):
                        for k in range(first, GROUP):
                            last = nc.tensor.matmul(bank[:, (k - first) * P:(k - first + 1) * P],
                                                    bc(of[:, bass.ds(w + k, 1)], [P, P]), S.ident_b[:],
                                                    start=True, stop=True)
                        last.then_inc(out, 1)

                spread(0, 0, 0)
                with pe.Fori(0, N_IT) as i:
                    blocks = window_blocks(nc, S, ET.PE, i)
                    for s in range(SLOTS):
                        q, g = s % 2, i * SLOTS + s
                        spread(g + 1, 1 - q, i * BODY + (s + 1) * GROUP)
                        pe.wait_ge(hot_made, g + MADE)
                        pe.wait_ge(scored, g + (SLOTS - 1))
                        for k in range(GROUP):
                            last = nc.tensor.matmul(
                                S.bank[6 + q][:, k * HEADS * parts:(k + 1) * HEADS * parts],
                                hot_t[:, q, k * P:(k + 1) * P],
                                er_parts[:].rearrange("p b h t -> p (b h t)")[
                                    :, bass.ds(blocks[s * GROUP + k] * (HEADS * parts), HEADS * parts)],
                                start=True, stop=True)
                        last.then_inc(er_out, 1)
                        pe.wait_ge(lo_made, g + MADE)
                        for k in range(LOOKED):
                            for n in range(parts):
                                last = nc.tensor.matmul(
                                    S.bank[4 + q][:, k * HEADS * NBLK:(k + 1) * HEADS * NBLK],
                                    hot_lo[:, q, k * P:(k + 1) * P],
                                    el_parts[:, n].rearrange("p h b -> p (h b)"),
                                    start=(n == 0), stop=(n == parts - 1))
                        last.then_inc(rows_out, 1)


def gat_softmax(nc, S, layer, M, score):
    ctx, sb, sem = scope(nc, f"gat_m{layer}")
    last = LINE - 1
    with ctx:
        line = sb("line", [P, HEADS, LINE])
        fwd, bwd = (sb(n, [P, 2, LINE]) for n in ("fwd", "bwd"))
        ends = sb("ends", [P, 2, HEADS])
        rows = sb("rows", [HEADS, 2, P])
        carry = sb("carry", [HEADS, 2, P])
        cols = sb("cols", [P, 2, HEADS])
        dved, relu, turned, taken = sem("dved"), sem("relu"), sem("turned"), sem("taken")
        ended, ends_out, carried, cols_out = sem("ended"), sem("ends_out"), sem("carried"), sem("cols_out")
        shifted, expd, back, written = sem("shifted"), sem("expd"), sem("back"), sem("written")
        by_column = score[:].rearrange("e (p j h) -> e j h p", j=WPP, h=HEADS)
        bank4 = lambda n: S.bank[n % 8][:].rearrange("p (h e) -> p h e", h=HEADS)
        with nc.Block() as block:

            @block.vector
            def _(dve):
                V = nc.vector
                st = Steps(dve, dved)
                V.scalar_tensor_tensor(out=score[:], in0=score[:], scalar=0.2, in1=score[:],
                                       op0=ALU.mult, op1=ALU.max).then_inc(relu, 1)
                st.mark(V.memset(rows[:], -BIG))
                for j in range(WPP):
                    dve.wait_ge(turned, j + 1)
                    V.tensor_copy(line[:, :, j * P:(j + 1) * P], bank4(j)).then_inc(taken, 1)
                dve.wait_ge(taken, WPP)
                for h in range(HEADS):
                    st.mark(V.tensor_tensor_scan(fwd[:, 0], M.keep_f[:], line[:, h], -BIG, ALU.add, ALU.max))
                    st.then(V.tensor_tensor_scan(bwd[:, 0, ::-1], M.keep_b[:, ::-1], line[:, h, ::-1], -BIG,
                                                 ALU.add, ALU.max))
                    V.tensor_copy(ends[:, 0, h:h + 1], fwd[:, 0, last:]).then_inc(ended, 1)
                    V.tensor_copy(ends[:, 1, h:h + 1], bwd[:, 0, 0:1]).then_inc(ended, 1)
                    dve.wait_ge(ended, 2 * (h + 1))
                dve.wait_ge(ends_out, 1)
                st.mark(V.tensor_tensor(rows[:, 0, 1:], S.bank[0][0:HEADS, 0:P - 1], M.join[:, 0, 1:], ALU.add))
                st.then(V.tensor_tensor(rows[:, 1, 0:P - 1], S.bank[0][0:HEADS, P + 1:2 * P], M.join[:, 1, 0:P - 1],
                                        ALU.add))
                V.tensor_tensor_scan(carry[:, 0], M.chain[:, 0], rows[:, 0], -BIG, ALU.add, ALU.max).then_inc(carried, 1)
                V.tensor_tensor_scan(carry[:, 1, ::-1], M.chain[:, 1, ::-1], rows[:, 1, ::-1], -BIG,
                                     ALU.add, ALU.max).then_inc(carried, 1)
                dve.wait_ge(cols_out, 1)
                st.then(V.tensor_copy(cols[:].rearrange("p k h -> p (k h)"), S.bank[1][:, 0:2 * HEADS]))
                for h in range(HEADS):
                    q = h % 2
                    st.mark(V.tensor_tensor_scan(fwd[:, q], M.keep_f[:], line[:, h], -BIG, ALU.add, ALU.max))
                    st.then(V.tensor_tensor_scan(bwd[:, q, ::-1], M.keep_b[:, ::-1], line[:, h, ::-1], -BIG,
                                                 ALU.add, ALU.max))
                    st.mark(V.scalar_tensor_tensor(out=fwd[:, q], in0=M.open_f[:], scalar=cols[:, 0, h:h + 1],
                                                   in1=fwd[:, q], op0=ALU.add, op1=ALU.max))
                    st.then(V.scalar_tensor_tensor(out=bwd[:, q], in0=M.open_b[:], scalar=cols[:, 1, h:h + 1],
                                                   in1=bwd[:, q], op0=ALU.add, op1=ALU.max))
                    st.then(V.tensor_tensor(fwd[:, q], fwd[:, q], bwd[:, q], ALU.max))
                    V.tensor_tensor(line[:, h], line[:, h], fwd[:, q], ALU.subtract).then_inc(shifted, 1)
                    dve.wait_ge(shifted, h + 1)
                for j in range(WPP):
                    dve.wait_ge(back, j + 1)
                    V.tensor_copy(by_column[:, j], bank4(j)).then_inc(written, 1)
                dve.wait_ge(written, WPP)

            @block.scalar
            def _(act):
                for h in range(HEADS):
                    act.wait_ge(shifted, h + 1)
                    nc.scalar.activation(line[:, h], line[:, h], ACT.Exp).then_inc(expd, 1)

            @block.tensor
            def _(pe):
                pe.wait_ge(relu, 1)
                for j in range(WPP):
                    if j >= 8:
                        pe.wait_ge(taken, j - 7)
                    for h in range(HEADS):
                        last_i = nc.tensor.transpose(S.bank[j % 8][:, h * P:(h + 1) * P], by_column[:, j, h], S.ident[:])
                    last_i.then_inc(turned, 1)
                pe.wait_ge(ended, 2 * HEADS)
                pe.wait_ge(taken, WPP)
                for k in range(2):
                    last_i = nc.tensor.transpose(S.bank[0][0:HEADS, k * P:(k + 1) * P], ends[:, k], S.ident[:])
                last_i.then_inc(ends_out, 1)
                pe.wait_ge(carried, 2)
                for k in range(2):
                    last_i = nc.tensor.transpose(S.bank[1][:, k * HEADS:(k + 1) * HEADS], carry[:, k],
                                                 S.ident[0:HEADS, 0:HEADS])
                last_i.then_inc(cols_out, 1)
                pe.wait_ge(expd, HEADS)
                for j in range(WPP):
                    if j >= 8:
                        pe.wait_ge(written, j - 7)
                    for h in range(HEADS):
                        last_i = nc.tensor.transpose(S.bank[j % 8][:, h * P:(h + 1) * P],
                                                     line[:, h, j * P:(j + 1) * P], S.ident[:])
                    last_i.then_inc(back, 1)


def gat_gather(nc, S, T, layer, score, acc):
    ctx, sb, sem = scope(nc, f"gat_g{layer}")
    with ctx:
        idx = sb("idx", [P, SLOTS, GROUP], I32)
        feat = sb("feat", [P, SLOTS, GROUP, D])
        weighted = sb("weighted", [P, 2, GROUP, ROW])
        hot = sb("hot", [P, 2, GROUP * P])
        cleared, idx_made, passed = sem("cleared"), sem("idx_made"), sem("passed")
        hot_made, weighed, sum_out, added = sem("hot_made"), sem("weighed"), sem("sum_out"), sem("added")
        got = [sem(f"got{s}") for s in range(SLOTS)]
        with nc.Block() as block:

            @block.gpsimd
            def _(pool):
                nc.gpsimd.memset(acc[:, 0:NB * ROW], 0.0).then_inc(cleared, 1)
                with pool.Fori(0, N_IT) as i:
                    for s in range(SLOTS):
                        pool.wait_ge(idx_made, i * SLOTS + (s + 1))
                        pool.sem_inc(passed, 1)
                        for k in range(GROUP):
                            nc.gpsimd.indirect_dma_start(
                                out=feat[:, s, k], out_offset=None, in_=T.feat,
                                in_offset=bass.IndirectOffsetOnAxis(ap=idx[:, s, k:k + 1].bitcast(U32), axis=0),
                            ).then_inc(got[s], 16)
                for s in range(SLOTS):
                    pool.wait_ge(got[s], N_IT * 16 * GROUP)

            @block.scalar
            def _(act):
                with act.Fori(0, N_IT) as i:
                    for s in range(SLOTS):
                        act.wait_ge(weighed, i * SLOTS + (s + 1))
                        act.sem_inc(passed, 1)
                        nc.scalar.copy(idx[:, s], S.src_i[:, bass.ds(i * BODY + s * GROUP, GROUP)]).then_inc(idx_made, 1)

            @block.vector
            def _(dve):
                V = nc.vector

                def weigh(i, s):
                    q, g, w = s % 2, i * SLOTS + s, i * BODY + s * GROUP
                    yield
                    dve.wait_ge(sum_out, g * GROUP + GROUP)
                    shape = [P, GROUP, P]
                    V.tensor_tensor(hot[:, q].rearrange("p (k n) -> p k n", k=GROUP),
                                    bc(S.rel_b[:, bass.ds(w, GROUP)].unsqueeze(2), shape),
                                    bc(S.row_b[:, None, :], shape), ALU.is_equal).then_inc(hot_made, 1)
                    yield
                    weight = score[:, bass.ds(w * HEADS, GROUP * HEADS)]
                    V.tensor_copy(weighted[:, q, :, D:ROW],
                                  weight.rearrange("p (k h) -> p k h", h=HEADS)).then_inc(hot_made, 1)
                    yield
                    dve.wait_ge(got[s], i * (16 * GROUP) + 16 * GROUP)
                    V.tensor_tensor(weighted[:, q, :, 0:D].rearrange("p k (h d) -> p k h d", d=HD),
                                    feat[:, s].rearrange("p k (h d) -> p k h d", d=HD),
                                    bc(weight.rearrange("p (k h) -> p k h", h=HEADS).unsqueeze(3),
                                       [P, GROUP, HEADS, HD]), ALU.mult).then_inc(weighed, 1)
                    yield

                def step(i, s, blocks, ahead):
                    n = i * BODY + s * GROUP
                    for k in range(GROUP):
                        next(ahead, None)
                        dve.wait_ge(sum_out, n + (k + 1 + 2 * GROUP))
                        dve.wait_ge(added, n + (k + 2 * GROUP))
                        to = acc[:, bass.ds(blocks[s * GROUP + k] * ROW, ROW)]
                        V.tensor_tensor(to, S.bank[s % 2 * GROUP + k][:, 0:ROW], to, ALU.add).then_inc(added, 1)

                dve.sem_inc(weighed, SLOTS)
                dve.wait_ge(cleared, 1)
                dve.sem_inc(added, 2 * GROUP)
                for _ in weigh(0, 0):
                    pass
                with dve.Fori(0, N_IT - 1) as i:
                    blocks = window_blocks(nc, S, ET.DVE, i)
                    for s in range(SLOTS):
                        step(i, s, blocks, weigh(i + (s + 1) // SLOTS, (s + 1) % SLOTS))
                i = N_IT - 1
                blocks = window_blocks(nc, S, ET.DVE, i)
                for s in range(SLOTS):
                    step(i, s, blocks, weigh(i, s + 1) if s + 1 < SLOTS else iter(()))
                dve.wait_ge(added, N_WIN + 2 * GROUP)

            @block.tensor
            def _(pe):
                pe.sem_inc(sum_out, 2 * GROUP)
                with pe.Fori(0, N_IT) as i:
                    for s in range(SLOTS):
                        q, g, n = s % 2, i * SLOTS + s, i * BODY + s * GROUP
                        pe.wait_ge(hot_made, g * 2 + 2)
                        pe.wait_ge(weighed, g + (1 + SLOTS))
                        for k in range(GROUP):
                            pe.wait_ge(added, n + (k + 1))
                            nc.tensor.matmul(S.bank[q * GROUP + k][:, 0:ROW], hot[:, q, k * P:(k + 1) * P],
                                             weighted[:, q, k], start=True, stop=True).then_inc(sum_out, 1)


def gat_finish(nc, S, layer, acc, h):
    ctx, sb, sem = scope(nc, f"gat_f{layer}")
    step = 5
    with ctx:
        inv = sb("inv", [P, NB * HEADS])
        neg = sb("neg", [P, 2, step * D])
        dved, divided, lowered, expd, done = sem("dved"), sem("divided"), sem("lowered"), sem("expd"), sem("done")
        by_row = acc[:, 0:NB * ROW].rearrange("p (b n) -> p b n", n=ROW)
        den = by_row[:, :, D:ROW]
        inv3 = inv[:].rearrange("p (b h) -> p b h", h=HEADS)
        chunks = NB // step
        with nc.Block() as block:

            @block.vector
            def _(dve):
                V = nc.vector
                st = Steps(dve, dved)
                st.then(V.tensor_scalar(inv3, den, 1.0 / BIG, None, ALU.max))
                st.then(V.reciprocal(inv3, inv3))
                with dve.Fori(0, NB) as b:
                    sums = acc[:, bass.ds(b * ROW, D)]
                    to = sums if layer == 2 else h[:, bass.ds(b * D, D)]
                    V.tensor_tensor(to.rearrange("p (h d) -> p h d", d=HD), sums.rearrange("p (h d) -> p h d", d=HD),
                                    bc(inv[:, bass.ds(b * HEADS, HEADS)].unsqueeze(2), [P, HEADS, HD]),
                                    ALU.mult).then_inc(divided, 1)
                dve.wait_ge(divided, NB)
                if layer == 2:
                    st.then(V.tensor_tensor(in_sbuf(h), in_sbuf(h), by_row[:, :, 0:D], ALU.add))

                def lower(c, q):
                    V.tensor_scalar(neg[:, q], h[:, bass.ds(c * (step * D), step * D)], 0.0, None,
                                    ALU.min).then_inc(lowered, 1)

                lower(0, 0)
                lower(1, 1)

                def finish(c, q):
                    at = h[:, bass.ds(c * (step * D), step * D)]
                    dve.wait_ge(expd, c + 1)
                    V.scalar_tensor_tensor(out=at, in0=at, scalar=0.0, in1=neg[:, q],
                                           op0=ALU.max, op1=ALU.add).then_inc(done, 1)
                    dve.wait_ge(done, c + 1)

                with dve.Fori(0, chunks // 2 - 1) as i:
                    for q in range(2):
                        finish(i * 2 + q, q)
                        lower(i * 2 + (q + 2), q)
                for q in range(2):
                    finish(chunks - 2 + q, q)
                st.then(V.tensor_scalar(h[:], h[:], -1.0, None, ALU.add))

            @block.scalar
            def _(act):
                with act.Fori(0, chunks // 2) as i:
                    for q in range(2):
                        act.wait_ge(lowered, i * 2 + (q + 1))
                        nc.scalar.activation(neg[:, q], neg[:, q], ACT.Exp).then_inc(expd, 1)


def move(nc, stage, pairs):
    ctx, sb, sem = scope(nc, stage)
    with ctx:
        moved = sem("moved")
        with nc.Block() as block:

            @block.sync
            def _(sp):
                for to, of in pairs:
                    sp.dma_start(to, of).then_inc(moved, 16)
                sp.wait_ge(moved, 16 * len(pairs))


def in_sbuf(t):
    return t[:].rearrange("p (b d) -> p b d", d=D)


def in_dram(t):
    return t.rearrange("(b p) d -> p b d", p=P)


def linear(nc, S, A, x, z):
    ctx, sb, sem = scope(nc, "linear")
    with ctx:
        weight = sb("weight", [P, 2, D])
        bias = sb("bias", [P, D])
        transposed_weight(nc, S, "linear_w", A["L1_ffn_weight"], weight)
        move(nc, "linear_b", [(bias[:], bc(A["L1_ffn_bias"].rearrange("(a d) -> a d", a=1), [P, D]))])

        def feed(V, b, rows):
            return V.tensor_copy(rows[:], z[:, bass.ds(b * D, D)])

        def posts(sb, sem):
            return [sb(f"t{q}", [P, D]) for q in range(2)], sem("biased")

        def post(V, dve, b, out, q, local):
            t, biased = local
            V.tensor_tensor(t[q][:], out, bias[:], ALU.add).then_inc(biased, 1)
            dve.wait_ge(biased, b + 1)
            at = x[:, bass.ds(b * D, D)]
            return V.tensor_tensor(at, at, t[q][:], ALU.add)

        project(nc, S, "linear_p", weight, D, feed, post, posts)


def build(nc, A, out):
    ctx = ExitStack()
    with ctx:
        def sb(name, shape, dt=FP32, c=ctx):
            return c.enter_context(nc.sbuf_tensor(name, shape, dt))

        def dram(name, shape, dt=FP32):
            return nc.dram_tensor(name, shape, dt, kind="Internal").ap()

        S, T = Shared(), Tables()
        S.ident, S.ones, S.lower, S.row = (sb(n, [P, P]) for n in ("ident", "ones", "lower", "row"))
        S.ident_b, S.lower_b, S.row_b, S.zero_b = (
            sb(n, [P, P], BF16) for n in ("ident_b", "lower_b", "row_b", "zero_b"))
        S.col, S.minus_col, S.dinv = sb("col", [P, 1]), sb("minus_col", [P, 1]), sb("dinv", [P, NB])
        S.bank = [ctx.enter_context(nc.psum_tensor(f"bank{i}", [P, 512], FP32)) for i in range(8)]
        T.edges = [dram("edge_src", (EDGE_ROWS * P,), I32), dram("edge_dst", (EDGE_ROWS * P,), I32)]
        T.blk = dram("blk_table", (WL,), I32)
        T.x, T.h, T.feat = (dram(n, (N_PAD, D)) for n in ("x_kept", "h_kept", "feat_table"))
        T.el = dram("el_table", (N_PAD, HEADS))
        T.acc = [dram(f"acc{k}", ((NB + 1) * P, D)) for k in range(GROUP)]
        constants(nc, S)
        with ExitStack() as edges:
            S.src_i, S.blk_row = sb("src_i", [P, WL], I32, edges), sb("blk_row", [1, WL], I32, edges)
            S.rel_b, S.lo_b, S.hi_b = (sb(n, [P, WL], BF16, edges) for n in ("rel_b", "lo_b", "hi_b"))
            M = Masks()
            M.keep_f, M.keep_b, M.open_f, M.open_b = (
                sb(n, [P, LINE], FP32, edges) for n in ("keep_f", "keep_b", "open_f", "open_b"))
            M.chain, M.join = (sb(n, [HEADS, 2, P], FP32, edges) for n in ("chain", "join"))
            with ExitStack() as part:
                S.key, S.src_m = (sb(n, [P, WL], FP32, part) for n in ("key", "src_m"))
                S.hi128_b = sb("hi128_b", [P, WL], BF16, part)
                with ExitStack() as one:
                    S.rel = sb("rel", [P, WL], FP32, one)
                    prep_edges(nc, S, T, A["src"], A["dst"])
                segment_masks(nc, S, M)
                degrees(nc, S)
                y = sb("y", [P, NB * D], FP32, part)
                load_nodes(nc, "load_y", A["x"], y)
                normalise(nc, S, "ln0", y, y, S.dinv)
                gcn_scatter(nc, S, T, y)
            with ExitStack() as part:
                x, z = (sb(n, [P, NB * D], FP32, part) for n in ("x", "z"))
                load_nodes(nc, "load_x", A["x"], x)
                gcn_out(nc, S, T, A, x, z)
                normalise(nc, S, "ln1", x, z)
                experts(nc, S, T, A, x, z)
                normalise(nc, S, "ln2", x, z)
                move(nc, "keep_x", [(in_dram(T.x), in_sbuf(x)), (in_dram(T.h), in_sbuf(z))])
            acc = sb("acc", [P, NB * WROW], FP32, edges)
            for layer in (1, 2):
                with ExitStack() as part:
                    h = sb(f"h{layer}", [P, NB * D], FP32, part)
                    move(nc, f"load_h{layer}", [(in_sbuf(h), in_dram(T.h))])
                    gat_tables(nc, S, T, A, layer, h, acc)
                with ExitStack() as part:
                    score = sb(f"score{layer}", [P, WL * HEADS], FP32, part)
                    gat_scores(nc, S, T, layer, acc, score)
                    gat_softmax(nc, S, layer, M, score)
                    gat_gather(nc, S, T, layer, score, acc)
                with ExitStack() as part:
                    h = sb(f"h_out{layer}", [P, NB * D], FP32, part)
                    if layer == 2:
                        move(nc, "load_res", [(in_sbuf(h), in_dram(T.h))])
                    gat_finish(nc, S, layer, acc, h)
                    move(nc, f"keep_h{layer}", [(in_dram(T.h), in_sbuf(h))])
        x, z = sb("x_end", [P, NB * D]), sb("z_end", [P, NB * D])
        move(nc, "back_x", [(in_sbuf(x), in_dram(T.x)), (in_sbuf(z), in_dram(T.h))])
        add_nodes(nc, x, z)
        normalise(nc, S, "ln3", x, z)
        linear(nc, S, A, x, z)
        full = (NBLK - 1) * P
        move(nc, "store", [(out[0:full, :].rearrange("(b p) d -> p b d", p=P), in_sbuf(x)[:, 0:NBLK - 1]),
                           (out[full:N, :], in_sbuf(x)[0:TAIL, NBLK - 1])])


def add_nodes(nc, x, z):
    ctx, sb, sem = scope(nc, "add")
    with ctx:
        added = sem("added")
        with nc.Block() as block:

            @block.vector
            def _(dve):
                nc.vector.tensor_tensor(x[:], x[:], z[:], ALU.add).then_inc(added, 1)
                dve.wait_ge(added, 1)


_INS = ["x", "src", "dst", "L0_gnn_W", "L0_gnn_b", "L0_ffn_Wr", "L0_ffn_br", "L0_ffn_W1", "L0_ffn_b1", "L0_ffn_W2",
        "L0_ffn_b2", "L0_ffn_gamma", "L0_ffn_beta", "L1_gnn_W1", "L1_gnn_al1", "L1_gnn_ar1", "L1_gnn_W2",
        "L1_gnn_al2", "L1_gnn_ar2", "L1_ffn_weight", "L1_ffn_bias"]


def kernel(**inputs):
    import numpy as _np
    import concourse.bacc as _bacc
    from concourse import mybir as _mybir
    from concourse.bass_utils import run_bass_kernel_spmd as _run

    nc = _bacc.Bacc("TRN2", target_bir_lowering=False, num_devices=1)
    arrays, args = {}, {}
    for name in _INS:
        a = _np.ascontiguousarray(inputs[name])
        arrays[f"in_{name}_dram"] = a
        args[name] = nc.dram_tensor(f"in_{name}_dram", a.shape, _mybir.dt.from_np(a.dtype), kind="ExternalInput").ap()
    out = nc.dram_tensor("out_0_dram", (N, D), _mybir.dt.float32, kind="ExternalOutput").ap()
    build(nc, args, out)
    r = _run(nc, [arrays], core_ids=[0])
    return r.results[0]["out_0_dram"]
```

```python
from contextlib import ExitStack

import concourse.bass as bass
from concourse import mybir

FP32, BF16, I32, U32 = mybir.dt.float32, mybir.dt.bfloat16, mybir.dt.int32, mybir.dt.uint32
ALU = mybir.AluOpType
ACT = mybir.ActivationFunctionType
AX = mybir.AxisListType
ET = mybir.EngineType

P = 128
N, D, E = 6250, 256, 200000
NBLK = -(-N // P)
NB = NBLK + 1
N_PAD = NB * P
HEADS, HD = 4, 64
GROUP = 4
SLOTS = 4
BODY = GROUP * SLOTS
N_WIN = -(-(E // P + 1 + NBLK) // BODY) * BODY
N_IT = N_WIN // BODY
WPP = -(-N_WIN // P)
WL = WPP * P
LINE = WPP * P
EDGE_ROWS = E // P + 4
START_MAX = E + 64
FAR = 8191.0
BIG = 1.0e30
RING = 2
MADE, ROOM = RING + 1, 1
RAW_P, RAW_C = 125, E // 125
EPS = 1e-5
TAIL = N - (NBLK - 1) * P
ROW = D + HEADS


class Shared:
    pass


class Tables:
    pass


class Steps:

    def __init__(self, engine, sem):
        self.engine, self.sem, self.n = engine, sem, 0

    def mark(self, ins):
        self.n += 1
        ins.then_inc(self.sem, 1)

    def then(self, ins):
        self.mark(ins)
        self.engine.wait_ge(self.sem, self.n)

    def wait(self):
        self.engine.wait_ge(self.sem, self.n)


def scope(nc, stage):
    ctx = ExitStack()
    sems = []

    def sem(name):
        sems.append(nc.alloc_semaphore(name=f"{stage}_{name}"))
        return sems[-1]

    def clear(error, *_):
        if error:
            return
        with nc.Block() as block:

            @block.gpsimd
            def _(pool):
                nc.clear_and_free_semaphores(sems)

    sb = lambda name, shape, dt=FP32: ctx.enter_context(nc.sbuf_tensor(f"{stage}_{name}", shape, dt))
    ctx.push(clear)
    return ctx, sb, sem


def bc(ap, shape):
    return ap.to_broadcast(shape)


def constants(nc, S):
    ctx, sb, sem = scope(nc, "const")
    with ctx:
        made, cast = sem("made"), sem("cast")
        with nc.Block() as block:

            @block.gpsimd
            def _(pool):
                st = Steps(pool, made)
                st.mark(nc.gpsimd.memset(S.ident[:], 0.0))
                st.mark(nc.gpsimd.memset(S.ones[:], 1.0))
                st.mark(nc.gpsimd.memset(S.lower[:], 1.0))
                st.mark(nc.gpsimd.iota(S.row[:], pattern=[[1, P]], base=0, channel_multiplier=0,
                                       allow_small_or_imprecise_dtypes=True))
                st.then(nc.gpsimd.iota(S.col[:], pattern=[[0, 1]], base=0, channel_multiplier=1,
                                       allow_small_or_imprecise_dtypes=True))
                st.mark(nc.gpsimd.affine_select(out=S.ident[:], in_=S.ident[:], compare_op=ALU.not_equal, fill=1.0,
                                                base=0, pattern=[[-1, P]], channel_multiplier=1))
                st.then(nc.gpsimd.affine_select(out=S.lower[:], in_=S.lower[:], compare_op=ALU.is_gt, fill=0.0,
                                                base=0, pattern=[[-1, P]], channel_multiplier=1))

            @block.vector
            def _(dve):
                dve.wait_ge(made, 7)
                nc.vector.tensor_copy(S.ident_b[:], S.ident[:]).then_inc(cast, 1)
                nc.vector.tensor_copy(S.lower_b[:], S.lower[:]).then_inc(cast, 1)
                nc.vector.tensor_copy(S.row_b[:], S.row[:]).then_inc(cast, 1)
                nc.vector.tensor_scalar(S.minus_col[:], S.col[:], -1.0, None, ALU.mult).then_inc(cast, 1)
                dve.wait_ge(cast, 4)


def prep_edges(nc, S, T, src, dst):
    ctx, sb, sem = scope(nc, "prep")
    with ctx:
        dst_i = sb("dst_i", [P, RAW_C], I32)
        dst_b = sb("dst_b", [P, RAW_C], BF16)
        junk = sb("junk", [P, RAW_C], BF16)
        thr = sb("thr", [P, NB])
        cnt = sb("cnt", [P, NB])
        pads = sb("pads", [8, 2, (EDGE_ROWS * P - E) // 8], I32)
        bs = sb("bs", [P, NB])
        nw = sb("nw", [P, NBLK])
        nwi = sb("nwi", [P, NBLK], I32)
        ws = sb("ws", [P, NB])
        zero = sb("zero", [P, LINE])
        off = sb("off", [P, NB])
        dof = sb("dof", [P, NBLK])
        wid = sb("wid", [P, WPP])
        cmp = sb("cmp", [P, WPP, NBLK])
        blk = sb("blk", [P, WPP])
        start = sb("start", [P, WPP])
        idx = sb("idx", [P, WPP], I32)
        blki = sb("blki", [P, WPP], I32)
        line_i = sb("line_i", [P, 2, LINE], I32)
        ls = sb("ls", [P, LINE])
        rel = sb("rel", [P, LINE])
        valid = sb("valid", [P, LINE])
        bw = sb("bw", [P, LINE])
        tmp = sb("tmp", [P, WL], I32)
        loaded, padded, dved = sem("loaded"), sem("padded"), sem("dve")
        dstd, counted, summed = sem("dstd"), sem("counted"), sem("summed")
        indexed, gathered, blocks = sem("indexed"), sem("gathered"), sem("blocks")
        lines, turned, taken = sem("lines"), sem("turned"), sem("taken")
        made, blkout, cnts = sem("made"), sem("blkout"), sem("cnts")

        with nc.Block() as block:

            @block.sync
            def _(sp):
                sp.dma_start(dst_i[0:RAW_P, :], dst.rearrange("(p c) -> p c", p=RAW_P)).then_inc(dstd, 16)
                for k, v in enumerate((src, dst)):
                    sp.dma_start(T.edges[k][0:E].rearrange("(p c) -> p c", p=RAW_P),
                                 v.rearrange("(p c) -> p c", p=RAW_P)).then_inc(loaded, 16)
                sp.wait_ge(made, 3)
                for k in range(2):
                    sp.dma_start(T.edges[k][E:EDGE_ROWS * P].rearrange("(p c) -> p c", p=8),
                                 pads[:, k, :]).then_inc(padded, 16)
                sp.wait_ge(blocks, 1)
                sp.dma_start(T.blk.rearrange("(p j) -> p j", j=WPP), blki[:]).then_inc(blkout, 16)
                sp.wait_ge(blkout, 16)
                sp.dma_start(S.blk_row[0:1, :], T.blk.rearrange("(a w) -> a w", a=1)).then_inc(blkout, 16)
                sp.wait_ge(blkout, 32)

            @block.gpsimd
            def _(pool):
                nc.gpsimd.memset(pads[:, 0, :], 0).then_inc(made, 1)
                nc.gpsimd.memset(pads[:, 1, :], int(FAR)).then_inc(made, 1)
                nc.gpsimd.iota(thr[:], pattern=[[1, NB]], base=0, channel_multiplier=0,
                               allow_small_or_imprecise_dtypes=True).then_inc(made, 1)
                nc.gpsimd.iota(wid[:], pattern=[[1, WPP]], base=0, channel_multiplier=WPP,
                               allow_small_or_imprecise_dtypes=True).then_inc(made, 1)
                nc.gpsimd.memset(zero[:], 0.0).then_inc(made, 1)
                pool.wait_ge(loaded, 32)
                pool.wait_ge(padded, 32)
                pool.wait_ge(indexed, 1)
                for k in range(2):
                    table = T.edges[k].rearrange("(r c) -> r c", c=P)
                    for j in range(WPP):
                        nc.gpsimd.indirect_dma_start(
                            out=line_i[:, k, j * P:(j + 1) * P], out_offset=None, in_=table,
                            in_offset=bass.IndirectOffsetOnAxis(ap=idx[:, j:j + 1].bitcast(U32), axis=1),
                        ).then_inc(gathered, 16)

            @block.vector
            def _(dve):
                st = Steps(dve, dved)
                V = nc.vector
                dve.wait_ge(dstd, 16)
                dve.wait_ge(made, 5)
                V.memset(cnt[:], 0.0).then_inc(cnts, 1)
                st.then(V.tensor_scalar(dst_i[0:RAW_P, :], dst_i[0:RAW_P, :], 7, None, ALU.arith_shift_right))
                st.then(V.tensor_copy(dst_b[0:RAW_P, :], dst_i[0:RAW_P, :]))
                step = 7
                with dve.Fori(0, NBLK // step) as i:
                    for k in range(1, step + 1):
                        b = i * step + k
                        dve.wait_ge(cnts, b)
                        V.tensor_scalar(junk[0:RAW_P, :], dst_b[0:RAW_P, :], thr[0:RAW_P, bass.ds(b, 1)], 0.0,
                                        ALU.is_lt, ALU.add, accum_out=cnt[0:RAW_P, bass.ds(b, 1)]).then_inc(cnts, 1)
                dve.wait_ge(cnts, NB)
                V.memset(off[:], 0.0).then_inc(counted, 1)
                dve.wait_ge(counted, 1)
                dve.wait_ge(summed, 1)
                st.then(V.tensor_copy(bs[:], S.bank[0][:, 0:NB]))
                st.then(V.tensor_tensor(nw[:], bs[:, 1:NB], bs[:, 0:NBLK], ALU.subtract))
                st.then(V.tensor_scalar(nw[:], nw[:], float(P - 1), None, ALU.add))
                st.then(V.tensor_copy(nwi[:], nw[:]))
                st.then(V.tensor_scalar(nwi[:], nwi[:], 7, None, ALU.arith_shift_right))
                st.then(V.tensor_copy(nw[:], nwi[:]))
                st.mark(V.memset(ws[:, 0:1], 0.0))
                st.then(V.tensor_tensor_scan(ws[:, 1:NB], zero[:, 0:NBLK], nw[:], 0.0, ALU.add, ALU.add))
                st.then(V.scalar_tensor_tensor(out=off[:], in0=ws[:], scalar=-float(P), in1=bs[:],
                                               op0=ALU.mult, op1=ALU.add))
                st.then(V.tensor_tensor(dof[:], off[:, 1:NB], off[:, 0:NBLK], ALU.subtract))
                shape = [P, WPP, NBLK]
                st.then(V.tensor_tensor(cmp[:], bc(ws[:, None, 1:NB], shape), bc(wid[:, :, None], shape), ALU.is_le))
                st.then(V.tensor_reduce(blk[:], cmp[:], AX.X, ALU.add))
                st.then(V.tensor_tensor(cmp[:], cmp[:], bc(dof[:, None, :], shape), ALU.mult))
                st.then(V.tensor_reduce(start[:], cmp[:], AX.X, ALU.add))
                st.then(V.scalar_tensor_tensor(out=start[:], in0=wid[:], scalar=float(P), in1=start[:],
                                               op0=ALU.mult, op1=ALU.add))
                st.then(V.tensor_scalar(start[:], start[:], float(START_MAX), None, ALU.min))
                V.tensor_copy(idx[:], start[:]).then_inc(indexed, 1)
                V.tensor_copy(blki[:], blk[:]).then_inc(blocks, 1)
                shape = [P, WPP, P]
                st.then(V.tensor_copy(bw[:].rearrange("p (j e) -> p j e", e=P), bc(blk[:, :, None], shape)))
                dve.wait_ge(gathered, 2 * 16 * WPP)
                st.mark(V.tensor_copy(ls[:], line_i[:, 0, :]))
                st.then(V.tensor_copy(S.key[:], line_i[:, 1, :]))
                st.then(V.scalar_tensor_tensor(out=rel[:], in0=bw[:], scalar=-float(P), in1=S.key[:],
                                               op0=ALU.mult, op1=ALU.add))
                st.mark(V.tensor_scalar(valid[:], rel[:], 0.0, None, ALU.is_ge))
                st.then(V.tensor_scalar(bw[:], rel[:], float(P), None, ALU.is_lt))
                st.then(V.tensor_tensor(valid[:], valid[:], bw[:], ALU.mult))
                for x, out in ((S.key, S.key), (rel, rel), (ls, bw)):
                    st.then(V.scalar_tensor_tensor(out=out[:], in0=x[:], scalar=1.0, in1=valid[:],
                                                   op0=ALU.add, op1=ALU.mult))
                    st.then(V.tensor_scalar(out[:], out[:], -1.0, None, ALU.add))
                V.memset(off[:], 0.0).then_inc(lines, 1)
                for n in range(3 * WPP):
                    k, j = divmod(n, WPP)
                    dve.wait_ge(turned, n + 1)
                    to = (S.src_i, S.rel, S.src_m)[k]
                    V.tensor_copy(to[:].rearrange("e (p j) -> e j p", j=WPP)[:, j, :],
                                  S.bank[1 + n % 7][:, 0:P]).then_inc(taken, 1)
                dve.wait_ge(taken, 3 * WPP)
                st.mark(V.tensor_copy(S.rel_b[:], S.rel[:]))
                st.then(V.tensor_copy(tmp[:], S.src_m[:]))
                st.then(V.tensor_scalar(line_i[:, 0, :], tmp[:], 7, None, ALU.arith_shift_right))
                st.then(V.tensor_scalar(tmp[:], tmp[:], P - 1, None, ALU.bitwise_and))
                st.mark(V.tensor_copy(S.lo_b[:], tmp[:]))
                st.then(V.tensor_copy(S.hi_b[:], line_i[:, 0, :]))
                st.then(V.tensor_scalar(S.hi128_b[:], S.hi_b[:], float(P), None, ALU.mult))

            @block.tensor
            def _(pe):
                pe.wait_ge(counted, 1)
                nc.tensor.matmul(S.bank[0][:, 0:NB], S.ones[:], cnt[:], start=True, stop=True).then_inc(summed, 1)
                pe.wait_ge(lines, 1)
                for n in range(3 * WPP):
                    k, j = divmod(n, WPP)
                    if n >= 7:
                        pe.wait_ge(taken, n - 6)
                    nc.tensor.transpose(S.bank[1 + n % 7][:, 0:P], (ls, rel, bw)[k][:, j * P:(j + 1) * P],
                                        S.ident[:]).then_inc(turned, 1)


def made2(h):
    return 2 * RING + h + 1


def room2(h):
    return h + 1


def window_blocks(nc, S, engine, i):
    _, blocks = nc.values_load_multi_w_load_instructions(
        S.blk_row[0:1, bass.ds(i * BODY, BODY)], engines=(engine,), min_val=0, max_val=NB - 1,
        skip_runtime_bounds_check_because="the table holds counts of at most NB - 1 blocks")
    return blocks


def degrees(nc, S):
    ctx, sb, sem = scope(nc, "deg")
    half = BODY // 2
    with ctx:
        rows = sb("rows", [P, P, half], BF16)
        hot_lo = sb("hot_lo", [P, 2, P, half], BF16)
        hot_hi = sb("hot_hi", [P, 2, NB, half], BF16)
        node = sb("node", [P, NB])
        deg = sb("deg", [P, NB])
        root = sb("root", [P, NB])
        made, ready, used, spread = sem("made"), sem("ready"), sem("used"), sem("spread")
        total, dved, rooted = sem("total"), sem("dved"), sem("rooted")
        sums = S.bank[0][:, 0:NB]
        with nc.Block() as block:

            @block.gpsimd
            def _(pool):
                nc.gpsimd.iota(node[:], pattern=[[P, NB]], base=0, channel_multiplier=1,
                               allow_small_or_imprecise_dtypes=True).then_inc(made, 1)
                nc.gpsimd.memset(S.zero_b[:], 0.0).then_inc(made, 1)

            @block.vector
            def _(dve):
                V = nc.vector
                V.tensor_copy(rows[:], bc(S.row[:].unsqueeze(2), [P, P, half])).then_inc(spread, 1)
                dve.wait_ge(spread, 1)
                with dve.Fori(0, N_IT) as i:
                    for h in range(2):
                        w = i * BODY + h * half
                        dve.wait_ge(used, i * 2 + (h + 1))
                        for hot, of, n in ((hot_lo, S.lo_b, P), (hot_hi, S.hi_b, NB)):
                            V.tensor_tensor(hot[:, h], bc(of[:, bass.ds(w, half)].unsqueeze(1), [P, n, half]),
                                            rows[:, 0:n], ALU.is_equal).then_inc(ready, 1)
                dve.wait_ge(total, 1)
                st = Steps(dve, dved)
                st.then(V.tensor_scalar(node[:], node[:], float(N), None, ALU.is_ge))
                st.then(V.tensor_tensor(deg[:], sums, node[:], ALU.add))
                dve.wait_ge(rooted, 1)
                st.then(V.reciprocal(S.dinv[:], root[:]))

            @block.scalar
            def _(act):
                act.wait_ge(dved, 2)
                nc.scalar.activation(root[:], deg[:], ACT.Sqrt).then_inc(rooted, 1)

            @block.tensor
            def _(pe):
                pe.sem_inc(used, 2)
                pe.wait_ge(made, 2)
                nc.tensor.matmul(sums, S.zero_b[:], S.zero_b[:, 0:NB], start=True, stop=False)
                with pe.Fori(0, N_IT) as i:
                    for h in range(2):
                        pe.wait_ge(ready, i * 4 + 2 * (h + 1))
                        for k in range(half):
                            last = nc.tensor.matmul(sums, hot_lo[:, h, :, k], hot_hi[:, h, :, k],
                                                    start=False, stop=False, skip_group_check=True)
                        last.then_inc(used, 1)
                nc.tensor.matmul(sums, S.zero_b[:], S.zero_b[:, 0:NB], start=False,
                                 stop=True).then_inc(total, 1)


def load_nodes(sp, x, into, cleared, loaded):
    full = (NBLK - 1) * P
    sp.dma_start(into[:, 0:(NBLK - 1) * D].rearrange("p (b d) -> p b d", d=D),
                 x[0:full, :].rearrange("(b p) d -> p b d", p=P)).then_inc(loaded, 16)
    sp.wait_ge(cleared, 1)
    sp.dma_start(into[0:TAIL, (NBLK - 1) * D:NBLK * D], x[full:N, :]).then_inc(loaded, 16)


def clear_tail(nc, into, cleared):
    nc.gpsimd.memset(into[:, (NBLK - 1) * D:NB * D], 0.0).then_inc(cleared, 1)


def start_load(nc, x, into, cleared, loaded):
    with nc.Block() as block:

        @block.gpsimd
        def _(pool):
            clear_tail(nc, into, cleared)

        @block.sync
        def _(sp):
            load_nodes(sp, x, into, cleared, loaded)


def arrived(nc, sem, count):
    with nc.Block() as block:

        @block.sync
        def _(sp):
            sp.wait_ge(sem, count)


def normalise(nc, stage, x, z, scale=None):
    ctx, sb, sem = scope(nc, stage)
    step = 5
    with ctx:
        stats = sb("stats", [P, NB, 6])
        mean = sb("mean", [P, NB])
        var = sb("var", [P, NB])
        rstd = sb("rstd", [P, NB])
        stated, dved, rooted, out = sem("stated"), sem("dved"), sem("rooted"), sem("out")
        flat = stats[:].rearrange("p b s -> p (b s)")
        with nc.Block() as block:

            @block.vector
            def _(dve):
                V = nc.vector
                st = Steps(dve, dved)
                with dve.Fori(0, NB // step) as i:
                    for k in range(step):
                        V.bn_stats(flat[:, bass.ds(i * (step * 6) + 6 * k, 6)],
                                   x[:, bass.ds(i * (step * D) + k * D, D)]).then_inc(stated, 1)
                dve.wait_ge(stated, NB)
                st.then(V.tensor_tensor(mean[:], stats[:, :, 1], stats[:, :, 4], ALU.add))
                st.then(V.tensor_tensor(var[:], stats[:, :, 1], stats[:, :, 4], ALU.subtract))
                st.then(V.tensor_tensor(var[:], var[:], var[:], ALU.mult))
                st.then(V.tensor_tensor(rstd[:], stats[:, :, 2], stats[:, :, 5], ALU.add))
                st.then(V.tensor_scalar(var[:], var[:], 0.25, EPS, ALU.mult, ALU.add))
                st.then(V.scalar_tensor_tensor(out=var[:], in0=rstd[:], scalar=1.0 / D, in1=var[:],
                                               op0=ALU.mult, op1=ALU.add))
                st.then(V.tensor_scalar(mean[:], mean[:], 0.5, None, ALU.mult))
                dve.wait_ge(rooted, 1)
                st.then(V.reciprocal(rstd[:], var[:]))
                if scale is not None:
                    st.then(V.tensor_tensor(rstd[:], rstd[:], scale[:], ALU.mult))
                with dve.Fori(0, NB // step) as i:
                    for k in range(step):
                        b = i * step + k
                        V.tensor_scalar(z[:, bass.ds(b * D, D)], x[:, bass.ds(b * D, D)], mean[:, bass.ds(b, 1)],
                                        rstd[:, bass.ds(b, 1)], ALU.subtract, ALU.mult).then_inc(out, 1)
                dve.wait_ge(out, NB)

            @block.scalar
            def _(act):
                act.wait_ge(dved, 6)
                nc.scalar.activation(var[:], var[:], ACT.Sqrt).then_inc(rooted, 1)


def clear_accumulators(nc, T, zero, cleared):
    ctx, _, sem = scope(nc, "clear")
    with ctx:
        made = sem("made")
        with nc.Block() as block:

            @block.gpsimd
            def _(pool):
                nc.gpsimd.memset(zero[:], 0.0).then_inc(made, 1)

            @block.sync
            def _(sp):
                sp.wait_ge(made, 1)
                for k in range(GROUP):
                    sp.dma_start(in_dram(T.acc[k])[:, 0:NB],
                                 bc(zero[:, None, :], [P, NB, D])).then_inc(cleared, 16)


def gcn_scatter(nc, S, T, y, zero, cleared):
    ctx, sb, sem = scope(nc, "gcn")
    with ctx:
        target = sb("target", [P, WL])
        spare = sb("spare", [P, 1])
        same = sb("same", [P, 2, GROUP * P], BF16)
        hot = sb("hot", [P, 2, GROUP * P], BF16)
        earlier = sb("earlier", [P, GROUP * P], BF16)
        n_earlier = sb("n_earlier", [P, GROUP])
        pick = sb("pick", [P, GROUP])
        idx = sb("idx", [P, SLOTS, GROUP], I32)
        spread = sb("spread", [P, 2, GROUP * P])
        msg = sb("msg", [P, SLOTS, GROUP, D])
        made, prep = sem("made"), sem("prep")
        src_out, same_made, hot_made = sem("src_out"), sem("same_made"), sem("hot_made")
        spread_out, spread_made = sem("spread_out"), sem("spread_made")
        msg_out, msg_made = sem("msg_out"), sem("msg_made")
        earlier_made, counted, picked, idx_made = sem("earlier_made"), sem("counted"), sem("picked"), sem("idx_made")
        landed, passed = sem("landed"), sem("passed")
        added = [sem(f"added{k}") for k in range(GROUP)]
        v4 = lambda t: t.rearrange("p (k e) -> p k e", k=GROUP)
        shape = [P, GROUP, P]
        with nc.Block() as block:

            @block.gpsimd
            def _(pool):
                nc.gpsimd.iota(spare[:], pattern=[[0, 1]], base=N_PAD, channel_multiplier=1,
                               allow_small_or_imprecise_dtypes=True).then_inc(made, 1)
                for k in range(GROUP):
                    pool.dma_start(in_dram(T.acc[k])[:, NB:],
                                   zero[:].unsqueeze(1)).then_inc(added[k], 16)
                pool.wait_ge(cleared, 16 * GROUP)
                pool.sem_inc(landed, SLOTS)
                with pool.Fori(0, N_IT) as i:
                    for s in range(SLOTS):
                        g = i * SLOTS + s
                        pool.wait_ge(idx_made, g + 1)
                        pool.wait_ge(msg_made, g * 2 + made2(1))
                        for k in range(GROUP):
                            pool.wait_ge(added[k], g * 16 + 16)
                            pool.sem_inc(landed if k == GROUP - 1 else passed, 1)
                            nc.gpsimd.indirect_dma_start(
                                out=T.acc[k], in_=msg[:, s, k], in_offset=None, compute_op=ALU.add,
                                out_offset=bass.IndirectOffsetOnAxis(ap=idx[:, s, k:k + 1].bitcast(U32), axis=0),
                            ).then_inc(added[k], 16)
                for k in range(GROUP):
                    pool.wait_ge(added[k], N_WIN // GROUP * 16 + 16)

            @block.vector
            def _(dve):
                V = nc.vector
                st = Steps(dve, prep)
                dve.sem_inc(same_made, RING)
                dve.wait_ge(made, 1)
                st.then(V.tensor_scalar(target[:], S.src_m[:], spare[:, 0:1], None, ALU.subtract))
                st.then(V.scalar_tensor_tensor(out=target[:], in0=S.src_m[:], scalar=0.0, in1=target[:],
                                               op0=ALU.is_ge, op1=ALU.mult))
                with dve.Fori(0, N_IT) as i:
                    for s in range(SLOTS):
                        q, g, w = s % 2, i * SLOTS + s, i * BODY + s * GROUP
                        dve.wait_ge(src_out, g + MADE)
                        dve.wait_ge(spread_out, g + ROOM)
                        V.tensor_tensor(v4(same[:, q]), v4(S.bank[q][:]),
                                        bc(S.src_m[:, bass.ds(w, GROUP)].unsqueeze(2), shape),
                                        ALU.is_equal).then_inc(same_made, 1)
                        V.tensor_tensor(v4(hot[:, q]), bc(S.rel_b[:, bass.ds(w, GROUP)].unsqueeze(2), shape),
                                        bc(S.row_b[:, None, :], shape), ALU.is_equal).then_inc(hot_made, 1)
                        dve.wait_ge(same_made, g + MADE)
                        V.tensor_tensor(v4(earlier[:]), v4(same[:, q]), bc(S.lower_b[:, None, :], shape),
                                        ALU.mult).then_inc(earlier_made, 1)
                        dve.wait_ge(earlier_made, g + 1)
                        V.tensor_reduce(n_earlier[:], v4(earlier[:]), AX.X, ALU.add).then_inc(counted, 1)
                        dve.wait_ge(counted, g + 1)
                        V.scalar_tensor_tensor(out=pick[:], in0=n_earlier[:], scalar=0.5,
                                               in1=target[:, bass.ds(w, GROUP)],
                                               op0=ALU.is_lt, op1=ALU.mult).then_inc(picked, 1)
                        dve.wait_ge(picked, g + 1)
                        dve.wait_ge(landed, g + 2)
                        V.tensor_scalar(idx[:, s], pick[:], spare[:, 0:1], None, ALU.add).then_inc(idx_made, 1)

            @block.scalar
            def _(act):
                act.sem_inc(spread_made, RING)
                act.sem_inc(msg_made, 2 * RING)
                with act.Fori(0, N_IT) as i:
                    for s in range(SLOTS):
                        q, g = s % 2, i * SLOTS + s
                        act.wait_ge(spread_out, g + MADE)
                        act.wait_ge(msg_out, g * 2 + room2(1))
                        nc.scalar.copy(spread[:, q], S.bank[2 + q][:]).then_inc(spread_made, 1)
                        act.wait_ge(landed, g + 2)
                        for h in range(2):
                            act.wait_ge(msg_out, g * 2 + made2(h))
                            nc.scalar.copy(msg[:, s, 2 * h:2 * h + 2].rearrange("p k d -> p (k d)"),
                                           S.bank[4 + 2 * q + h][:]).then_inc(msg_made, 1)

            @block.tensor
            def _(pe):
                def sources(g, q, w):
                    pe.wait_ge(same_made, g + ROOM)
                    pe.sem_inc(passed, 1)
                    for k in range(GROUP):
                        to = S.bank[q][:, k * P:(k + 1) * P]
                        nc.tensor.matmul(to, bc(S.lo_b[:, bass.ds(w + k, 1)], [P, P]), S.ident_b[:],
                                         start=True, stop=False)
                        last = nc.tensor.matmul(to, bc(S.hi128_b[:, bass.ds(w + k, 1)], [P, P]), S.ident_b[:],
                                                start=False, stop=True)
                    last.then_inc(src_out, 1)

                pe.sem_inc(src_out, RING)
                pe.sem_inc(spread_out, RING)
                pe.sem_inc(msg_out, 2 * RING)
                sources(0, 0, 0)
                with pe.Fori(0, N_IT) as i:
                    blocks = window_blocks(nc, S, ET.PE, i)
                    for s in range(SLOTS):
                        q, g, w = s % 2, i * SLOTS + s, i * BODY + s * GROUP
                        sources(g + 1, 1 - q, w + GROUP)
                        pe.wait_ge(hot_made, g + 1)
                        pe.wait_ge(same_made, g + MADE)
                        pe.wait_ge(spread_made, g + ROOM)
                        for k in range(GROUP):
                            e = slice(k * P, (k + 1) * P)
                            last = nc.tensor.matmul(S.bank[2 + q][:, e], hot[:, q, e], same[:, q, e],
                                                    start=True, stop=True)
                        last.then_inc(spread_out, 1)
                        pe.wait_ge(spread_made, g + MADE)
                        for h in range(2):
                            pe.wait_ge(msg_made, g * 2 + room2(h))
                            for k in (2 * h, 2 * h + 1):
                                last = nc.tensor.matmul(
                                    S.bank[4 + 2 * q + h][:, (k % 2) * D:(k % 2 + 1) * D],
                                    spread[:, q, k * P:(k + 1) * P],
                                    y[:, bass.ds(blocks[s * GROUP + k] * D, D)], start=True, stop=True)
                            last.then_inc(msg_out, 1)


def transposed_weight(nc, S, stage, w, into):
    ctx, sb, sem = scope(nc, stage)
    with ctx:
        rows = sb("rows", [P, 2, D])
        loaded, turned, taken = sem("loaded"), sem("turned"), sem("taken")
        with nc.Block() as block:

            @block.sync
            def _(sp):
                sp.dma_start(rows[:], w.rearrange("(o p) i -> p o i", p=P)).then_inc(loaded, 16)

            @block.tensor
            def _(pe):
                pe.wait_ge(loaded, 16)
                for c in range(2):
                    for o in range(2):
                        last = nc.tensor.transpose(S.bank[c][:, o * P:(o + 1) * P], rows[:, o, c * P:(c + 1) * P],
                                                   S.ident[:])
                last.then_inc(turned, 1)

            @block.vector
            def _(dve):
                dve.wait_ge(turned, 1)
                for c in range(2):
                    nc.vector.tensor_copy(into[:, c, 0:D], S.bank[c][:, 0:D]).then_inc(taken, 1)
                dve.wait_ge(taken, 2)


def project(nc, S, stage, weight, cols, feed, post, posts, loads=None):
    ctx, sb, sem = scope(nc, stage)
    with ctx:
        rows = [sb(f"rows{q}", [P, D]) for q in range(2)]
        turned = [sb(f"turned{q}", [P, 2, P]) for q in range(2)]
        fed, turn_out, turn_made = sem("fed"), sem("turn_out"), sem("turn_made")
        prod_out, done = sem("prod_out"), sem("done")
        local = posts(sb, sem)
        with nc.Block() as block:
            if loads:
                loads(block)

            @block.vector
            def _(dve):
                def feed_block(b, q):
                    dve.wait_ge(turn_out, b + ROOM)
                    feed(nc.vector, dve, b, rows[q]).then_inc(fed, 1)

                def post_block(b, q):
                    dve.wait_ge(prod_out, b + MADE)
                    post(nc.vector, dve, b, S.bank[2 + q][:, 0:cols], q, local).then_inc(done, 1)

                dve.sem_inc(done, RING)
                feed_block(0, 0)
                feed_block(1, 1)
                with dve.Fori(0, NB // 2 - 1) as i:
                    for q in range(2):
                        feed_block(i * 2 + (q + 2), q)
                        post_block(i * 2 + q, q)
                for q in range(2):
                    post_block(NB - 2 + q, q)
                dve.wait_ge(done, NB + RING)

            @block.scalar
            def _(act):
                act.sem_inc(turn_made, RING)
                with act.Fori(0, NB // 2) as i:
                    for q in range(2):
                        b = i * 2 + q
                        act.wait_ge(turn_out, b + MADE)
                        act.wait_ge(prod_out, b + ROOM)
                        nc.scalar.copy(turned[q][:].rearrange("p c n -> p (c n)"),
                                       S.bank[q][:, 0:2 * P]).then_inc(turn_made, 1)

            @block.tensor
            def _(pe):
                def turn(b, q):
                    pe.wait_ge(fed, b + 1)
                    pe.wait_ge(turn_made, b + ROOM)
                    for c in range(2):
                        last = nc.tensor.transpose(S.bank[q][:, c * P:(c + 1) * P], rows[q][:, c * P:(c + 1) * P],
                                                   S.ident[:])
                    last.then_inc(turn_out, 1)

                def multiply(b, q):
                    pe.wait_ge(turn_made, b + MADE)
                    pe.wait_ge(done, b + ROOM)
                    for c in range(2):
                        last = nc.tensor.matmul(S.bank[2 + q][:, 0:cols], turned[q][:, c, :], weight[:, c, 0:cols],
                                                start=(c == 0), stop=(c == 1))
                    last.then_inc(prod_out, 1)

                pe.sem_inc(turn_out, RING)
                pe.sem_inc(prod_out, RING)
                turn(0, 0)
                with pe.Fori(0, NB // 2 - 1) as i:
                    for q in range(2):
                        turn(i * 2 + (q + 1), 1 - q)
                        multiply(i * 2 + q, q)
                turn(NB - 1, 1)
                multiply(NB - 2, 0)
                multiply(NB - 1, 1)


def gcn_out(nc, S, T, A, x, y):
    ctx, sb, sem = scope(nc, "gcn_out")
    with ctx:
        weight = sb("weight", [P, 2, D])
        bias = sb("bias", [P, D])
        loaded, blocks_in, cleared, x_in = sem("loaded"), sem("blocks_in"), sem("cleared"), sem("x_in")
        chunk = 5
        summed = [sem(f"summed{c}") for c in range(NB // chunk)]
        transposed_weight(nc, S, "gcn_w", A["L0_gnn_W"], weight)
        with nc.Block() as block:

            @block.sync
            def _(sp):
                sp.dma_start(bias[:], bc(A["L0_gnn_b"].rearrange("(a d) -> a d", a=1), [P, D])).then_inc(loaded, 16)
                sp.wait_ge(loaded, 16)

        def loads(block):

            @block.sync
            def _(sp):
                load_nodes(sp, A["x"], x, cleared, x_in)

            @block.gpsimd
            def _(pool):
                clear_tail(nc, x, cleared)
                for t in range(len(summed) + GROUP):
                    for k in reversed(range(GROUP + 1)):
                        c = t - k
                        if not 0 <= c < len(summed):
                            continue
                        if k:
                            pool.wait_ge(summed[c], 16 * k)
                        if k == GROUP:
                            pool.sem_inc(blocks_in, chunk)
                            continue
                        pool.dma_start(in_sbuf(y)[:, c * chunk:(c + 1) * chunk],
                                       in_dram(T.acc[k][0:N_PAD, :])[:, c * chunk:(c + 1) * chunk],
                                       accum_op=ALU.add).then_inc(summed[c], 16)

        def feed(V, dve, b, rows):
            dve.wait_ge(blocks_in, b + 1)
            return V.tensor_scalar(rows[:], y[:, bass.ds(b * D, D)], S.dinv[:, bass.ds(b, 1)], None, ALU.mult)

        def posts(sb, sem):
            return [sb(f"t{q}", [P, D]) for q in range(2)], sem("biased")

        def post(V, dve, b, out, q, local):
            t, biased = local
            V.tensor_tensor(t[q][:], out, bias[:], ALU.add).then_inc(biased, 1)
            dve.wait_ge(biased, b + 1)
            dve.wait_ge(x_in, 32)
            return V.scalar_tensor_tensor(out=x[:, bass.ds(b * D, D)], in0=t[q][:], scalar=0.0,
                                          in1=x[:, bass.ds(b * D, D)], op0=ALU.max, op1=ALU.add)

        project(nc, S, "gcn_proj", weight, D, feed, post, posts, loads)


N_EXP, TOP_K, F = 8, 2, 512
FC = F // P
CAPACITY = -(-(N * 5) // (4 * N_EXP))


def route(nc, S, A, z, top_w, top_i):
    ctx, sb, sem = scope(nc, "route")
    with ctx:
        in_tail = sb("in_tail", [P, P])
        wr = sb("wr", [P, 2, N_EXP])
        br = sb("br", [P, N_EXP])
        mean = sb("mean", [P, D])
        mean_t = sb("mean_t", [P, 2, P])
        r, e, load = (sb(n, [P, N_EXP]) for n in ("r", "e", "load"))
        one = sb("one", [P, 1])
        best = sb("best", [P, 8])
        loaded, made, dved, expd = sem("loaded"), sem("made"), sem("dved"), sem("expd")
        summed, turned, multiplied, meaned, mean_turned = (
            sem(n) for n in ("summed", "turned", "multiplied", "meaned", "mean_turned"))
        with nc.Block() as block:

            @block.sync
            def _(sp):
                sp.dma_start(wr[:], A["L0_ffn_Wr"].rearrange("(c p) e -> p c e", p=P)).then_inc(loaded, 16)
                sp.dma_start(br[:], bc(A["L0_ffn_br"].rearrange("(a e) -> a e", a=1), [P, N_EXP])).then_inc(loaded, 16)

            @block.gpsimd
            def _(pool):
                nc.gpsimd.memset(in_tail[:], 1.0).then_inc(made, 1)
                pool.wait_ge(made, 1)
                nc.gpsimd.affine_select(out=in_tail[:], in_=in_tail[:], compare_op=ALU.is_gt, fill=0.0,
                                        base=TAIL, pattern=[[0, P]], channel_multiplier=-1).then_inc(made, 1)

            @block.tensor
            def _(pe):
                total = S.bank[0][:, 0:D]
                nc.tensor.matmul(total, S.ones[:], z[:, 0:D], start=True, stop=False)
                with pe.Fori(1, NBLK - 1) as b:
                    nc.tensor.matmul(total, S.ones[:], z[:, bass.ds(b * D, D)], start=False, stop=False,
                                     skip_group_check=True)
                pe.wait_ge(made, 2)
                nc.tensor.matmul(total, in_tail[:], z[:, (NBLK - 1) * D:NBLK * D], start=False,
                                 stop=True).then_inc(summed, 1)
                pe.wait_ge(meaned, 1)
                for c in range(2):
                    last = nc.tensor.transpose(S.bank[1][:, c * P:(c + 1) * P], mean[:, c * P:(c + 1) * P], S.ident[:])
                last.then_inc(turned, 1)
                pe.wait_ge(mean_turned, 1)
                pe.wait_ge(loaded, 32)
                for c in range(2):
                    last = nc.tensor.matmul(S.bank[2][:, 0:N_EXP], mean_t[:, c, :], wr[:, c, :],
                                            start=(c == 0), stop=(c == 1))
                last.then_inc(multiplied, 1)

            @block.scalar
            def _(act):
                for k in range(2):
                    act.wait_ge(made, 3 + k)
                    nc.scalar.activation(e[:], r[:], ACT.Exp).then_inc(expd, 1)
                act.wait_ge(made, 5)
                nc.scalar.activation(top_w[:, 1:2], top_w[:, 1:2], ACT.Exp).then_inc(expd, 1)

            @block.vector
            def _(dve):
                V = nc.vector
                st = Steps(dve, dved)

                def softmax(k):
                    st.then(V.tensor_reduce(one[:], r[:], AX.X, ALU.max))
                    V.tensor_scalar(r[:], r[:], one[:, 0:1], None, ALU.subtract).then_inc(made, 1)
                    dve.wait_ge(expd, k + 1)
                    st.then(V.tensor_reduce(one[:], e[:], AX.X, ALU.add))
                    st.then(V.reciprocal(one[:], one[:]))
                    st.then(V.tensor_scalar(r[:], e[:], one[:, 0:1], None, ALU.mult))

                dve.wait_ge(summed, 1)
                V.tensor_scalar(mean[:], S.bank[0][:, 0:D], 1.0 / N, None, ALU.mult).then_inc(meaned, 1)
                dve.wait_ge(turned, 1)
                V.tensor_copy(mean_t[:].rearrange("p c n -> p (c n)"), S.bank[1][:, 0:D]).then_inc(mean_turned, 1)
                dve.wait_ge(multiplied, 1)
                dve.wait_ge(loaded, 32)
                dve.wait_ge(made, 2)
                st.then(V.tensor_tensor(r[:], S.bank[2][:, 0:N_EXP], br[:], ALU.add))
                softmax(0)
                st.then(V.tensor_scalar(load[:], r[:], float(N), None, ALU.mult))
                st.then(V.reciprocal(load[:], load[:]))
                st.then(V.tensor_scalar(load[:], load[:], float(CAPACITY), 1.0, ALU.mult, ALU.min))
                st.then(V.tensor_tensor(r[:], r[:], load[:], ALU.mult))
                softmax(1)
                st.then(V.max(best[:], r[:]))
                st.then(V.max_index(top_i[:], best[:], r[:]))
                V.tensor_tensor(top_w[:, 1:2], best[:, 1:2], best[:, 0:1], ALU.subtract).then_inc(made, 1)
                dve.wait_ge(expd, 3)
                st.then(V.tensor_scalar(one[:], top_w[:, 1:2], 1.0, None, ALU.add))
                st.then(V.reciprocal(top_w[:, 0:1], one[:]))
                st.then(V.tensor_tensor(top_w[:, 1:2], top_w[:, 1:2], top_w[:, 0:1], ALU.mult))


def experts(nc, S, A, x, z):
    ctx, sb, sem = scope(nc, "ffn")
    with ctx:
        top_w = sb("top_w", [P, TOP_K])
        top_i = sb("top_i", [P, 8], U32)
        w1 = sb("w1", [P, TOP_K, 2, F])
        w2 = sb("w2", [P, TOP_K, FC, D])
        b1 = sb("b1", [P, TOP_K, FC])
        b2 = sb("b2", [P, TOP_K, D])
        route(nc, S, A, z, top_w, top_i)
        gamma, beta = sb("gamma", [P, D]), sb("beta", [P, D])
        loaded, scaled, b2_made, fetched = sem("loaded"), sem("scaled"), sem("b2_made"), sem("fetched")
        with nc.Block() as block:

            @block.sync
            def _(sp):
                for j in range(TOP_K):
                    e = sp.value_load(top_i[0:1, j:j + 1].bitcast(I32), min_val=0, max_val=N_EXP - 1)
                    pick = lambda name: A[name][bass.ds(e, 1)]
                    for to, of in (
                        (w1[:, j], pick("L0_ffn_W1").rearrange("a (c p) f -> p (a c) f", p=P)),
                        (w2[:, j], pick("L0_ffn_W2").rearrange("a (c p) d -> p (a c) d", p=P)),
                        (b1[:, j], pick("L0_ffn_b1").rearrange("a (c p) -> p (a c)", p=P)),
                        (b2[:, j], bc(pick("L0_ffn_b2"), [P, D])),
                    ):
                        sp.dma_start(to, of, allow_slow_non_contiguous=True).then_inc(loaded, 16)
                for to, name in ((gamma, "L0_ffn_gamma"), (beta, "L0_ffn_beta")):
                    sp.dma_start(to[:], bc(A[name].rearrange("(a d) -> a d", a=1), [P, D])).then_inc(fetched, 16)
                sp.wait_ge(loaded, 16 * 4 * TOP_K)
                sp.wait_ge(fetched, 32)

            @block.vector
            def _(dve):
                V = nc.vector
                dve.wait_ge(loaded, 16 * 4 * TOP_K)
                for j in range(TOP_K):
                    V.tensor_scalar(w2[:, j], w2[:, j], top_w[:, j:j + 1], None, ALU.mult).then_inc(scaled, 1)
                    V.tensor_scalar(b2[:, j], b2[:, j], top_w[:, j:j + 1], None, ALU.mult).then_inc(scaled, 1)
                dve.wait_ge(scaled, 2 * TOP_K)
                V.tensor_tensor(b2[:, 0], b2[:, 0], b2[:, 1], ALU.add).then_inc(b2_made, 1)
                dve.wait_ge(b2_made, 1)

        H = TOP_K * FC
        HB = H // 2
        rows = [sb(f"rows{q}", [P, 2, D]) for q in range(2)]
        turned = [sb(f"turned{q}", [P, 2, 2 * P]) for q in range(2)]
        hidden = [sb(f"hidden{q}", [P, H, 2 * P]) for q in range(2)]
        fed, turn_out, turn_made = sem("fed"), sem("turn_out"), sem("turn_made")
        hidden_out, hidden_made = sem("hidden_out"), sem("hidden_made")
        prod_out, done, shifted, biased = sem("prod_out"), sem("done"), sem("shifted"), sem("biased")
        PAIRS = NB // 2
        turn_bank, hidden_bank, prod_bank = S.bank[0], S.bank[1:5], S.bank[5:7]

        def pairs(engine, body):
            with engine.Fori(0, PAIRS // 2) as i:
                body(i * 2, 0)
                body(i * 2 + 1, 1)
            body(PAIRS - 1, 0)

        with nc.Block() as block:

            @block.vector
            def _(dve):
                V = nc.vector

                def feed(u, q):
                    dve.wait_ge(turn_out, u + ROOM)
                    at = z[:, bass.ds(u * (2 * D), 2 * D)]
                    V.tensor_copy(rows[q][:].rearrange("p k d -> p (k d)"), at).then_inc(fed, 1)
                    dve.wait_ge(fed, u + 1)
                    at = at.rearrange("p (k d) -> p k d", d=D)
                    V.tensor_tensor(at, at, bc(b2[:, 0:1, :], [P, 2, D]), ALU.add).then_inc(biased, 1)

                def post(u, q):
                    dve.wait_ge(biased, u + 1)
                    for k in range(2):
                        dve.wait_ge(prod_out, u * 2 + made2(k))
                        at = z[:, bass.ds(u * (2 * D) + k * D, D)]
                        V.tensor_tensor(at, prod_bank[k][:, 0:D], at, ALU.add).then_inc(done, 1)
                        at = x[:, bass.ds(u * (2 * D) + k * D, D)]
                        V.tensor_tensor(at, at, beta[:], ALU.add).then_inc(shifted, 1)

                dve.sem_inc(done, 2)
                feed(0, 0)
                feed(1, 1)
                with dve.Fori(0, PAIRS // 2 - 1) as i:
                    for q in range(2):
                        feed(i * 2 + (q + 2), q)
                        post(i * 2 + q, q)
                feed(PAIRS - 1, 0)
                post(PAIRS - 3, 0)
                post(PAIRS - 2, 1)
                post(PAIRS - 1, 0)
                dve.wait_ge(done, NB + 2)
                dve.wait_ge(shifted, NB)

            @block.scalar
            def _(act):
                def body(u, q):
                    act.wait_ge(turn_out, u + MADE)
                    act.wait_ge(hidden_out, u * HB + HB)
                    nc.scalar.copy(turned[q][:].rearrange("p c n -> p (c n)"), turn_bank[:]).then_inc(turn_made, 1)
                    act.wait_ge(prod_out, u * 2 + room2(1))
                    for n in range(HB):
                        act.wait_ge(hidden_out, u * HB + (n + 1 + 2 * HB))
                        for h in (2 * n, 2 * n + 1):
                            last = nc.scalar.activation(
                                hidden[q][:, h, :], hidden_bank[n][:, h % 2 * D:(h % 2 + 1) * D], ACT.Gelu,
                                bias=b1[:, h // FC, h % FC:h % FC + 1])
                        last.then_inc(hidden_made, 1)

                act.sem_inc(hidden_made, HB)
                pairs(act, body)

            @block.tensor
            def _(pe):
                def turn(u, q):
                    pe.wait_ge(fed, u + 1)
                    for c in range(2):
                        for k in range(2):
                            last = nc.tensor.transpose(turn_bank[:, (2 * c + k) * P:(2 * c + k + 1) * P],
                                                       rows[q][:, k, c * P:(c + 1) * P], S.ident[:])
                    last.then_inc(turn_out, 1)

                def hide(u, q):
                    pe.wait_ge(turn_made, u + 1)
                    for h in range(H):
                        j, f = divmod(h, FC)
                        if h % 2 == 0:
                            pe.wait_ge(hidden_made, u * HB + (h // 2 + 1))
                        for c in range(2):
                            last = nc.tensor.matmul(hidden_bank[h // 2][:, h % 2 * D:(h % 2 + 1) * D],
                                                    w1[:, j, c, f * P:(f + 1) * P], turned[q][:, c, :],
                                                    start=(c == 0), stop=(c == 1))
                        if h % 2:
                            last.then_inc(hidden_out, 1)

                def combine(u, q):
                    pe.wait_ge(hidden_made, u * HB + 2 * HB)
                    for k in range(2):
                        pe.wait_ge(done, u * 2 + (k + 1))
                        to = prod_bank[k][:, 0:D]
                        for h in range(H):
                            last = nc.tensor.matmul(to, hidden[q][:, h, k * P:(k + 1) * P], w2[:, h // FC, h % FC, :],
                                                    start=(h == 0), stop=(h == H - 1))
                        last.then_inc(prod_out, 1)

                pe.sem_inc(turn_out, RING)
                pe.sem_inc(hidden_out, 2 * HB)
                pe.sem_inc(prod_out, 2 * RING)
                turn(0, 0)
                hide(0, 0)
                turn(1, 1)
                with pe.Fori(0, PAIRS // 2 - 1) as i:
                    for q in range(2):
                        hide(i * 2 + (q + 1), 1 - q)
                        turn(i * 2 + (q + 2), q)
                        combine(i * 2 + q, q)
                hide(PAIRS - 2, 1)
                turn(PAIRS - 1, 0)
                combine(PAIRS - 3, 0)
                hide(PAIRS - 1, 0)
                combine(PAIRS - 2, 1)
                combine(PAIRS - 1, 0)

        normalise(nc, "ffn_ln", z, z)
        dved = sem("dved")
        with nc.Block() as block:

            @block.vector
            def _(dve):
                V = nc.vector
                st = Steps(dve, dved)
                view = lambda t: t[:].rearrange("p (b d) -> p b d", d=D)
                st.then(V.tensor_tensor(view(z), view(z), bc(gamma[:, None, :], [P, NB, D]), ALU.mult))
                st.then(V.tensor_tensor(x[:], x[:], z[:], ALU.add))


class Masks:
    pass


def segment_masks(nc, S, M):
    ctx, sb, sem = scope(nc, "masks")
    last = LINE - 1
    with ctx:
        ends = sb("ends", [P, 4, HEADS])
        rows = sb("rows", [HEADS, 4, P])
        link = sb("link", [HEADS, 2, P])
        zero = sb("zero", [P, LINE])
        cols = sb("cols", [P, 2, HEADS])
        dved, ended, turned, linked, cols_out, runs, runs_out = (
            sem(n) for n in ("dved", "ended", "turned", "linked", "cols_out", "runs", "runs_out"))
        with nc.Block() as block:

            @block.tensor
            def _(pe):
                pe.wait_ge(ended, 2)
                for k in range(2):
                    last_i = nc.tensor.transpose(S.bank[0][0:HEADS, k * P:(k + 1) * P], ends[:, k], S.ident[:])
                last_i.then_inc(turned, 1)
                pe.wait_ge(linked, 2)
                for k in range(2):
                    last_i = nc.tensor.transpose(S.bank[1][:, k * HEADS:(k + 1) * HEADS], link[:, k],
                                                 S.ident[0:HEADS, 0:HEADS])
                last_i.then_inc(cols_out, 1)
                pe.wait_ge(runs, 2)
                for k in range(2):
                    last_i = nc.tensor.transpose(S.bank[2][0:HEADS, k * P:(k + 1) * P], ends[:, 2 + k], S.ident[:])
                last_i.then_inc(runs_out, 1)

            @block.vector
            def _(dve):
                V = nc.vector
                st = Steps(dve, dved)
                V.tensor_copy(ends[:, 0], bc(S.key[:, 0:1], [P, HEADS])).then_inc(ended, 1)
                V.tensor_copy(ends[:, 1], bc(S.key[:, last:], [P, HEADS])).then_inc(ended, 1)
                st.mark(V.memset(zero[:], 0.0))
                st.then(V.memset(link[:], 0.0))
                dve.wait_ge(turned, 1)
                st.then(V.tensor_copy(rows[:, 0:2].rearrange("h k p -> h (k p)"), S.bank[0][0:HEADS, 0:2 * P]))
                V.tensor_tensor(link[:, 0, 1:], rows[:, 0, 1:], rows[:, 1, 0:P - 1], ALU.is_equal).then_inc(linked, 1)
                V.tensor_tensor(link[:, 1, 0:P - 1], rows[:, 0, 1:], rows[:, 1, 0:P - 1],
                                ALU.is_equal).then_inc(linked, 1)
                dve.wait_ge(cols_out, 1)
                st.then(V.tensor_copy(cols[:].rearrange("p k h -> p (k h)"), S.bank[1][:, 0:2 * HEADS]))
                st.mark(V.tensor_tensor(M.keep_f[:, 1:], S.key[:, 1:], S.key[:, 0:last], ALU.is_equal))
                st.mark(V.tensor_tensor(M.keep_b[:, 0:last], S.key[:, 1:], S.key[:, 0:last], ALU.is_equal))
                st.mark(V.tensor_copy(M.keep_f[:, 0:1], cols[:, 0, 0:1]))
                st.then(V.tensor_copy(M.keep_b[:, last:], cols[:, 1, 0:1]))
                st.then(V.tensor_tensor_scan(M.open_f[:], M.keep_f[:], zero[:], 1.0, ALU.mult, ALU.add))
                st.then(V.tensor_tensor_scan(M.open_b[:, ::-1], M.keep_b[:, ::-1], zero[:], 1.0, ALU.mult, ALU.add))
                V.tensor_copy(ends[:, 2], bc(M.open_f[:, last:], [P, HEADS])).then_inc(runs, 1)
                V.tensor_copy(ends[:, 3], bc(M.open_b[:, 0:1], [P, HEADS])).then_inc(runs, 1)
                st.mark(V.memset(M.keep_f[:, 0:1], 0.0))
                st.mark(V.memset(M.keep_b[:, last:], 0.0))
                dve.wait_ge(runs, 2)
                dve.wait_ge(runs_out, 1)
                st.mark(V.memset(M.chain[:], 0.0))
                st.mark(V.tensor_copy(M.join[:], link[:]))
                st.then(V.tensor_copy(rows[:, 2:4].rearrange("h k p -> h (k p)"), S.bank[2][0:HEADS, 0:2 * P]))
                st.mark(V.tensor_tensor(M.chain[:, 0, 1:], link[:, 0, 1:], rows[:, 2, 0:P - 1], ALU.mult))
                st.then(V.tensor_tensor(M.chain[:, 1, 0:P - 1], link[:, 1, 0:P - 1], rows[:, 3, 1:], ALU.mult))
                for t in (M.keep_f, M.keep_b, M.open_f, M.open_b, M.chain, M.join):
                    st.mark(V.tensor_scalar(t[:], t[:], -1.0, BIG, ALU.add, ALU.mult))
                st.wait()


WROW = D + 2 * HEADS


def gat_tables(nc, S, T, A, layer, z, table, feat_kept):
    ctx, sb, sem = scope(nc, f"gat_t{layer}")
    with ctx:
        weight = sb("weight", [P, 2, WROW])
        attn = sb("attn", [P, 2, D])
        prod = sb("prod", [P, 2, 2, D])
        loaded, multiplied, reduced, stored = sem("loaded"), sem("multiplied"), sem("reduced"), sem("stored")
        with nc.Block() as block:

            @block.sync
            def _(sp):
                sp.dma_start(weight[:, :, 0:D],
                             A[f"L1_gnn_W{layer}"].rearrange("(c p) n -> p c n", p=P)).then_inc(loaded, 16)
                for k, side in enumerate("lr"):
                    row = A[f"L1_gnn_a{side}{layer}"].rearrange("h d -> (h d)").rearrange("(a n) -> a n", a=1)
                    sp.dma_start(attn[:, k], bc(row, [P, D])).then_inc(loaded, 16)

            @block.vector
            def _(dve):
                dve.wait_ge(loaded, 48)
                for k in range(2):
                    nc.vector.tensor_tensor(prod[:, k], weight[:, :, 0:D], bc(attn[:, k:k + 1, :], [P, 2, D]),
                                            ALU.mult).then_inc(multiplied, 1)
                dve.wait_ge(multiplied, 2)
                for k in range(2):
                    nc.vector.tensor_reduce(weight[:, :, D + k * HEADS:D + (k + 1) * HEADS],
                                            prod[:, k].rearrange("p c (h d) -> p c h d", h=HEADS),
                                            AX.X, ALU.add).then_inc(reduced, 1)
                dve.wait_ge(reduced, 2)

        def feed(V, dve, b, rows):
            return V.tensor_copy(rows[:], z[:, bass.ds(b * D, D)])

        def post(V, dve, b, out, q, local):
            return V.tensor_copy(table[:, bass.ds(b * WROW, WROW)], out)

        project(nc, S, f"gat_p{layer}", weight, WROW, feed, post, lambda sb, sem: None)
        view = table[:, 0:NB * WROW].rearrange("p (b n) -> p b n", n=WROW)
        with nc.Block() as block:

            @block.sync
            def _(sp):
                sp.dma_start(in_dram(T.el), view[:, :, D:D + HEADS]).then_inc(stored, 16)
                sp.dma_start(in_dram(T.feat), view[:, :, 0:D]).then_inc(feat_kept, 16)
                sp.wait_ge(stored, 16)


LOOKED = 2
GATHERED = GROUP - LOOKED


def gat_scores(nc, S, T, layer, table, score):
    ctx, sb, sem = scope(nc, f"gat_s{layer}")
    n_idx, n_looked, parts = GROUP * HEADS, LOOKED * HEADS, 3
    with ctx:
        parted = sb("parted", [P, parts, NB, 2 * HEADS], BF16)
        rest = sb("rest", [P, NB, 2 * HEADS])
        el_parts = sb("el_parts", [P, parts, HEADS, NBLK], BF16)
        er_parts = sb("er_parts", [P, NB, HEADS, parts], BF16)
        idx = sb("idx", [P, SLOTS, GATHERED], I32)
        el = sb("el", [P, SLOTS, n_idx])
        er = sb("er", [P, 2, n_idx])
        far = sb("far", [P, GROUP * P], BF16)
        hot_lo = sb("hot_lo", [P, 2, LOOKED * P], BF16)
        hot_hi = sb("hot_hi", [P, 2, LOOKED, NBLK], BF16)
        hot_t = sb("hot_t", [P, 2, GROUP * P], BF16)
        rows = sb("rows", [P, LOOKED, HEADS, NBLK])
        cleared, idx_made, passed, split = sem("cleared"), sem("idx_made"), sem("passed"), sem("split")
        rel_out, lo_out, far_made, lo_made = sem("rel_out"), sem("lo_out"), sem("far_made"), sem("lo_made")
        hot_made, hi_made, er_out, rows_out = sem("hot_made"), sem("hi_made"), sem("er_out"), sem("rows_out")
        masked, er_made, el_made, scored = sem("masked"), sem("er_made"), sem("el_made"), sem("scored")
        got = [sem(f"got{s}") for s in range(SLOTS)]
        with nc.Block() as block:

            @block.gpsimd
            def _(pool):
                nc.gpsimd.memset(score[:, N_WIN * HEADS:], 0.0).then_inc(cleared, 1)
                with pool.Fori(0, N_IT) as i:
                    for s in range(SLOTS):
                        pool.wait_ge(idx_made, i * SLOTS + (s + 1))
                        pool.sem_inc(passed, 1)
                        for k in range(GATHERED):
                            nc.gpsimd.indirect_dma_start(
                                out=el[:, s, k * HEADS:(k + 1) * HEADS], out_offset=None, in_=T.el,
                                in_offset=bass.IndirectOffsetOnAxis(ap=idx[:, s, k:k + 1].bitcast(U32), axis=0),
                            ).then_inc(got[s], 16)
                for s in range(SLOTS):
                    pool.wait_ge(got[s], N_IT * 16 * GATHERED)

            @block.scalar
            def _(act):
                def indices(g, s, w):
                    act.wait_ge(scored, g + 1)
                    act.sem_inc(passed, 1)
                    nc.scalar.copy(idx[:, s], S.src_i[:, bass.ds(w, GATHERED)]).then_inc(idx_made, 1)

                act.sem_inc(hot_made, RING)
                act.sem_inc(far_made, RING)
                indices(0, 0, 0)
                indices(1, 1, GROUP)
                with act.Fori(0, N_IT) as i:
                    for s in range(SLOTS):
                        q, g = s % 2, i * SLOTS + s
                        indices(g + 2, (s + 2) % SLOTS, i * BODY + (s + 2) * GROUP)
                        act.wait_ge(rel_out, g + MADE)
                        act.wait_ge(hot_made, g + RING)
                        nc.scalar.activation(far[:], S.bank[q][:], ACT.Abs,
                                             bias=S.minus_col[:, 0:1]).then_inc(far_made, 1)
                        act.wait_ge(far_made, g + MADE)
                        act.wait_ge(er_out, g + ROOM)
                        nc.scalar.activation(hot_t[:, q], far[:], ACT.Relu, bias=1.0,
                                             scale=-1.0).then_inc(hot_made, 1)

            @block.vector
            def _(dve):
                V = nc.vector
                st = Steps(dve, split)
                st.then(V.tensor_copy(rest[:], table[:, 0:NB * WROW].rearrange("p (b n) -> p b n", n=WROW)[:, :, D:]))
                for n in range(parts):
                    st.then(V.tensor_copy(parted[:, n], rest[:]))
                    if n < parts - 1:
                        st.then(V.tensor_tensor(rest[:], rest[:], parted[:, n], ALU.subtract))
                for n in range(parts):
                    by_head = parted[:, n].rearrange("p b h -> p h b")
                    st.mark(V.tensor_copy(el_parts[:, n], by_head[:, 0:HEADS, 0:NBLK]))
                    st.mark(V.tensor_copy(er_parts[:, :, :, n], parted[:, n, :, HEADS:]))
                st.wait()
                dve.sem_inc(lo_made, RING)
                dve.sem_inc(scored, SLOTS)

                def hot(g, q):
                    dve.wait_ge(lo_out, g + MADE)
                    dve.wait_ge(rows_out, g + ROOM)
                    V.tensor_scalar(hot_lo[:, q], S.bank[2 + q][:, 0:LOOKED * P], S.col[:, 0:1], None,
                                    ALU.is_equal).then_inc(lo_made, 1)

                def hot_his(q, w):
                    shape = [P, LOOKED, NBLK]
                    V.tensor_tensor(hot_hi[:, q], bc(S.hi_b[:, bass.ds(w + GATHERED, LOOKED)].unsqueeze(2), shape),
                                    bc(S.row_b[:, None, 0:NBLK], shape), ALU.is_equal).then_inc(hi_made, 1)

                hot(0, 0)
                hot_his(0, 0)
                with dve.Fori(0, N_IT) as i:
                    for s in range(SLOTS):
                        q, g = s % 2, i * SLOTS + s
                        hot(g + 1, 1 - q)
                        dve.wait_ge(hi_made, g + 1)
                        dve.wait_ge(rows_out, g + MADE)
                        V.tensor_tensor(rows[:], S.bank[4 + q][:, 0:n_looked * NBLK].rearrange(
                            "p (k h b) -> p k h b", k=LOOKED, h=HEADS),
                            bc(hot_hi[:, q].unsqueeze(2), [P, LOOKED, HEADS, NBLK]), ALU.mult).then_inc(masked, 1)
                        dve.wait_ge(er_out, g + MADE)
                        V.tensor_reduce(er[:, q], S.bank[6 + q][:, 0:n_idx * parts].rearrange(
                            "p (n t) -> p n t", t=parts), AX.X, ALU.add).then_inc(er_made, 1)
                        dve.wait_ge(masked, g + 1)
                        V.tensor_reduce(el[:, s, GATHERED * HEADS:], rows[:].rearrange("p k h b -> p (k h) b"),
                                        AX.X, ALU.add).then_inc(el_made, 1)
                        hot_his(1 - q, i * BODY + (s + 1) * GROUP)
                        dve.wait_ge(el_made, g + 1)
                        dve.wait_ge(er_made, g + 1)
                        dve.wait_ge(got[s], i * (16 * GATHERED) + 16 * GATHERED)
                        V.tensor_tensor(score[:, bass.ds(i * (BODY * HEADS) + s * n_idx, n_idx)],
                                        er[:, q], el[:, s], ALU.add).then_inc(scored, 1)
                dve.wait_ge(cleared, 1)
                dve.wait_ge(lo_made, N_IT * SLOTS + MADE)
                dve.wait_ge(hi_made, N_IT * SLOTS + 1)
                dve.wait_ge(scored, N_IT * SLOTS + SLOTS)

            @block.tensor
            def _(pe):
                pe.sem_inc(rel_out, RING)
                pe.sem_inc(lo_out, RING)
                pe.sem_inc(er_out, RING)
                pe.sem_inc(rows_out, RING)

                def spread(g, q, w):
                    pe.wait_ge(far_made, g + ROOM)
                    pe.wait_ge(lo_made, g + ROOM)
                    pe.sem_inc(passed, 1)
                    for bank, of, first, out in ((S.bank[q], S.rel_b, 0, rel_out),
                                                 (S.bank[2 + q], S.lo_b, GATHERED, lo_out)):
                        for k in range(first, GROUP):
                            last = nc.tensor.matmul(bank[:, (k - first) * P:(k - first + 1) * P],
                                                    bc(of[:, bass.ds(w + k, 1)], [P, P]), S.ident_b[:],
                                                    start=True, stop=True)
                        last.then_inc(out, 1)

                spread(0, 0, 0)
                with pe.Fori(0, N_IT) as i:
                    blocks = window_blocks(nc, S, ET.PE, i)
                    for s in range(SLOTS):
                        q, g = s % 2, i * SLOTS + s
                        spread(g + 1, 1 - q, i * BODY + (s + 1) * GROUP)
                        pe.wait_ge(lo_made, g + MADE)
                        pe.wait_ge(scored, g + (SLOTS - 1))
                        for k in range(LOOKED):
                            for n in range(parts):
                                last = nc.tensor.matmul(
                                    S.bank[4 + q][:, k * HEADS * NBLK:(k + 1) * HEADS * NBLK],
                                    hot_lo[:, q, k * P:(k + 1) * P],
                                    el_parts[:, n].rearrange("p h b -> p (h b)"),
                                    start=(n == 0), stop=(n == parts - 1))
                        last.then_inc(rows_out, 1)
                        pe.wait_ge(hot_made, g + MADE)
                        for k in range(GROUP):
                            last = nc.tensor.matmul(
                                S.bank[6 + q][:, k * HEADS * parts:(k + 1) * HEADS * parts],
                                hot_t[:, q, k * P:(k + 1) * P],
                                er_parts[:].rearrange("p b h t -> p (b h t)")[
                                    :, bass.ds(blocks[s * GROUP + k] * (HEADS * parts), HEADS * parts)],
                                start=True, stop=True)
                        last.then_inc(er_out, 1)


def gat_softmax(nc, S, layer, M, score, scratch):
    ctx, sb, sem = scope(nc, f"gat_m{layer}")
    last = LINE - 1
    with ctx:
        by_head = lambda t, n: t[:, n * LINE:(n + HEADS) * LINE].rearrange("p (h e) -> p h e", e=LINE)
        line, bwd, fwd = by_head(scratch, 0), by_head(scratch, HEADS), by_head(score, 0)
        ends = sb("ends", [P, 2, HEADS])
        rows = sb("rows", [HEADS, 2, P])
        carry = sb("carry", [HEADS, 2, P])
        cols = sb("cols", [P, 2, HEADS])
        dved, relu, turned, taken, scanned = (sem(n) for n in ("dved", "relu", "turned", "taken", "scanned"))
        ended, ends_out, carried, cols_out = sem("ended"), sem("ends_out"), sem("carried"), sem("cols_out")
        shifted, expd, back, written = sem("shifted"), sem("expd"), sem("back"), sem("written")
        by_column = score[:].rearrange("e (p j h) -> e j h p", j=WPP, h=HEADS)
        bank4 = lambda n: S.bank[n % 8][:].rearrange("p (h e) -> p h e", h=HEADS)
        with nc.Block() as block:

            @block.vector
            def _(dve):
                V = nc.vector
                st = Steps(dve, dved)
                V.scalar_tensor_tensor(out=score[:], in0=score[:], scalar=0.2, in1=score[:],
                                       op0=ALU.mult, op1=ALU.max).then_inc(relu, 1)
                st.mark(V.memset(rows[:], -BIG))
                for j in range(WPP):
                    dve.wait_ge(turned, j + 1)
                    V.tensor_copy(line[:, :, j * P:(j + 1) * P], bank4(j)).then_inc(taken, 1)
                dve.wait_ge(taken, WPP)
                for h in range(HEADS):
                    V.tensor_tensor_scan(fwd[:, h], M.keep_f[:], line[:, h], -BIG,
                                         ALU.add, ALU.max).then_inc(scanned, 1)
                    V.tensor_tensor_scan(bwd[:, h, ::-1], M.keep_b[:, ::-1], line[:, h, ::-1], -BIG,
                                         ALU.add, ALU.max).then_inc(scanned, 1)
                dve.wait_ge(scanned, 2 * HEADS)
                V.tensor_copy(ends[:, 0], fwd[:, :, last]).then_inc(ended, 1)
                V.tensor_copy(ends[:, 1], bwd[:, :, 0]).then_inc(ended, 1)
                dve.wait_ge(ends_out, 1)
                st.mark(V.tensor_tensor(rows[:, 0, 1:], S.bank[0][0:HEADS, 0:P - 1], M.join[:, 0, 1:], ALU.add))
                st.then(V.tensor_tensor(rows[:, 1, 0:P - 1], S.bank[0][0:HEADS, P + 1:2 * P], M.join[:, 1, 0:P - 1],
                                        ALU.add))
                V.tensor_tensor_scan(carry[:, 0], M.chain[:, 0], rows[:, 0], -BIG,
                                     ALU.add, ALU.max).then_inc(carried, 1)
                V.tensor_tensor_scan(carry[:, 1, ::-1], M.chain[:, 1, ::-1], rows[:, 1, ::-1], -BIG,
                                     ALU.add, ALU.max).then_inc(carried, 1)
                dve.wait_ge(cols_out, 1)
                st.then(V.tensor_copy(cols[:].rearrange("p k h -> p (k h)"), S.bank[1][:, 0:2 * HEADS]))
                for h in range(HEADS):
                    st.mark(V.scalar_tensor_tensor(out=fwd[:, h], in0=M.open_f[:], scalar=cols[:, 0, h:h + 1],
                                                   in1=fwd[:, h], op0=ALU.add, op1=ALU.max))
                    st.then(V.scalar_tensor_tensor(out=bwd[:, h], in0=M.open_b[:], scalar=cols[:, 1, h:h + 1],
                                                   in1=bwd[:, h], op0=ALU.add, op1=ALU.max))
                    st.then(V.tensor_tensor(fwd[:, h], fwd[:, h], bwd[:, h], ALU.max))
                    V.tensor_tensor(line[:, h], line[:, h], fwd[:, h], ALU.subtract).then_inc(shifted, 1)
                dve.wait_ge(shifted, HEADS)
                for j in range(WPP):
                    dve.wait_ge(back, j + 1)
                    V.tensor_copy(by_column[:, j], bank4(j)).then_inc(written, 1)
                dve.wait_ge(written, WPP)

            @block.scalar
            def _(act):
                for h in range(HEADS):
                    act.wait_ge(shifted, h + 1)
                    nc.scalar.activation(line[:, h], line[:, h], ACT.Exp).then_inc(expd, 1)

            @block.tensor
            def _(pe):
                pe.wait_ge(relu, 1)
                for j in range(WPP):
                    if j >= 8:
                        pe.wait_ge(taken, j - 7)
                    for h in range(HEADS):
                        last_i = nc.tensor.transpose(S.bank[j % 8][:, h * P:(h + 1) * P], by_column[:, j, h],
                                                     S.ident[:])
                    last_i.then_inc(turned, 1)
                pe.wait_ge(ended, 2)
                pe.wait_ge(taken, WPP)
                for k in range(2):
                    last_i = nc.tensor.transpose(S.bank[0][0:HEADS, k * P:(k + 1) * P], ends[:, k], S.ident[:])
                last_i.then_inc(ends_out, 1)
                pe.wait_ge(carried, 2)
                for k in range(2):
                    last_i = nc.tensor.transpose(S.bank[1][:, k * HEADS:(k + 1) * HEADS], carry[:, k],
                                                 S.ident[0:HEADS, 0:HEADS])
                last_i.then_inc(cols_out, 1)
                pe.wait_ge(expd, HEADS)
                for j in range(WPP):
                    if j >= 8:
                        pe.wait_ge(written, j - 7)
                    for h in range(HEADS):
                        last_i = nc.tensor.transpose(S.bank[j % 8][:, h * P:(h + 1) * P],
                                                     line[:, h, j * P:(j + 1) * P], S.ident[:])
                    last_i.then_inc(back, 1)


def gat_gather(nc, S, T, layer, score, acc):
    ctx, sb, sem = scope(nc, f"gat_g{layer}")
    with ctx:
        idx = sb("idx", [P, SLOTS, GROUP], I32)
        feat = sb("feat", [P, SLOTS, GROUP, D])
        weighted = sb("weighted", [P, 2, GROUP, ROW])
        hot = sb("hot", [P, 2, GROUP * P])
        cleared, idx_made, passed = sem("cleared"), sem("idx_made"), sem("passed")
        hot_made, weighed, sum_out, added = sem("hot_made"), sem("weighed"), sem("sum_out"), sem("added")
        weights_in = sem("weights_in")
        got = [sem(f"got{s}") for s in range(SLOTS)]
        with nc.Block() as block:

            @block.gpsimd
            def _(pool):
                with pool.Fori(0, N_IT) as i:
                    for s in range(SLOTS):
                        pool.wait_ge(idx_made, i * SLOTS + (s + 1))
                        pool.sem_inc(passed, 1)
                        for k in range(GROUP):
                            nc.gpsimd.indirect_dma_start(
                                out=feat[:, s, k], out_offset=None, in_=T.feat,
                                in_offset=bass.IndirectOffsetOnAxis(ap=idx[:, s, k:k + 1].bitcast(U32), axis=0),
                            ).then_inc(got[s], 16)
                for s in range(SLOTS):
                    pool.wait_ge(got[s], N_IT * 16 * GROUP)

            @block.scalar
            def _(act):
                with act.Fori(0, N_IT) as i:
                    for s in range(SLOTS):
                        act.wait_ge(weighed, i * SLOTS + (s + 1))
                        act.sem_inc(passed, 1)
                        w = i * BODY + s * GROUP
                        nc.scalar.copy(idx[:, s], S.src_i[:, bass.ds(w, GROUP)]).then_inc(idx_made, 1)
                        act.wait_ge(sum_out, (i * SLOTS + s) * GROUP + GROUP)
                        act.sem_inc(passed, 1)
                        nc.scalar.copy(weighted[:, s % 2, :, D:ROW],
                                       score[:, bass.ds(w * HEADS, GROUP * HEADS)].rearrange(
                                           "p (k h) -> p k h", h=HEADS)).then_inc(weights_in, 1)

            @block.vector
            def _(dve):
                V = nc.vector

                def make_hot(i, s):
                    dve.wait_ge(sum_out, (i * SLOTS + s) * GROUP + GROUP)
                    shape = [P, GROUP, P]
                    V.tensor_tensor(hot[:, s % 2].rearrange("p (k n) -> p k n", k=GROUP),
                                    bc(S.rel_b[:, bass.ds(i * BODY + s * GROUP, GROUP)].unsqueeze(2), shape),
                                    bc(S.row_b[:, None, :], shape), ALU.is_equal).then_inc(hot_made, 1)

                def weigh(i, s):
                    weight = score[:, bass.ds((i * BODY + s * GROUP) * HEADS, GROUP * HEADS)]
                    dve.wait_ge(got[s], i * (16 * GROUP) + 16 * GROUP)
                    V.tensor_tensor(weighted[:, s % 2, :, 0:D].rearrange("p k (h d) -> p k h d", d=HD),
                                    feat[:, s].rearrange("p k (h d) -> p k h d", d=HD),
                                    bc(weight.rearrange("p (k h) -> p k h", h=HEADS).unsqueeze(3),
                                       [P, GROUP, HEADS, HD]), ALU.mult).then_inc(weighed, 1)

                def step(i, s, blocks, ahead):
                    n = i * BODY + s * GROUP
                    for k in range(GROUP):
                        if ahead and k == 1:
                            make_hot(*ahead)
                        if ahead and k == 2:
                            weigh(*ahead)
                        dve.wait_ge(sum_out, n + (k + 1 + 2 * GROUP))
                        dve.wait_ge(added, n + (k + 2 * GROUP))
                        to = acc[:, bass.ds(blocks[s * GROUP + k] * ROW, ROW)]
                        V.tensor_tensor(to, S.bank[s % 2 * GROUP + k][:, 0:ROW], to, ALU.add).then_inc(added, 1)

                dve.sem_inc(weighed, SLOTS)
                V.memset(acc[:, 0:NB * ROW], 0.0).then_inc(cleared, 1)
                dve.wait_ge(cleared, 1)
                dve.sem_inc(added, 2 * GROUP)
                make_hot(0, 0)
                weigh(0, 0)
                with dve.Fori(0, N_IT - 1) as i:
                    blocks = window_blocks(nc, S, ET.DVE, i)
                    for s in range(SLOTS):
                        step(i, s, blocks, (i + (s + 1) // SLOTS, (s + 1) % SLOTS))
                i = N_IT - 1
                blocks = window_blocks(nc, S, ET.DVE, i)
                for s in range(SLOTS):
                    step(i, s, blocks, (i, s + 1) if s + 1 < SLOTS else None)
                dve.wait_ge(added, N_WIN + 2 * GROUP)

            @block.tensor
            def _(pe):
                pe.sem_inc(sum_out, 2 * GROUP)
                with pe.Fori(0, N_IT) as i:
                    for s in range(SLOTS):
                        q, g, n = s % 2, i * SLOTS + s, i * BODY + s * GROUP
                        pe.wait_ge(hot_made, g + 1)
                        pe.wait_ge(weights_in, g + 1)
                        pe.wait_ge(weighed, g + (1 + SLOTS))
                        for k in range(GROUP):
                            pe.wait_ge(added, n + (k + 1))
                            nc.tensor.matmul(S.bank[q * GROUP + k][:, 0:ROW], hot[:, q, k * P:(k + 1) * P],
                                             weighted[:, q, k], start=True, stop=True).then_inc(sum_out, 1)


def gat_finish(nc, layer, acc, h):
    ctx, sb, sem = scope(nc, f"gat_f{layer}")
    step = 5
    with ctx:
        inv = sb("inv", [P, NB * HEADS])
        neg = sb("neg", [P, 2, step * D])
        dved, divided, lowered, expd, done = sem("dved"), sem("divided"), sem("lowered"), sem("expd"), sem("done")
        by_row = acc[:, 0:NB * ROW].rearrange("p (b n) -> p b n", n=ROW)
        den = by_row[:, :, D:ROW]
        inv3 = inv[:].rearrange("p (b h) -> p b h", h=HEADS)
        chunks = NB // step
        with nc.Block() as block:

            @block.vector
            def _(dve):
                V = nc.vector
                st = Steps(dve, dved)
                st.then(V.tensor_scalar(inv3, den, 1.0 / BIG, None, ALU.max))
                st.then(V.reciprocal(inv3, inv3))
                with dve.Fori(0, chunks) as i:
                    for k in range(step):
                        sums = acc[:, bass.ds(i * (step * ROW) + k * ROW, D)]
                        to = sums if layer == 2 else h[:, bass.ds(i * (step * D) + k * D, D)]
                        V.tensor_tensor(
                            to.rearrange("p (h d) -> p h d", d=HD), sums.rearrange("p (h d) -> p h d", d=HD),
                            bc(inv[:, bass.ds(i * (step * HEADS) + k * HEADS, HEADS)].unsqueeze(2), [P, HEADS, HD]),
                            ALU.mult).then_inc(divided, 1)
                dve.wait_ge(divided, NB)
                if layer == 2:
                    st.then(V.tensor_tensor(in_sbuf(h), in_sbuf(h), by_row[:, :, 0:D], ALU.add))

                def lower(c, q):
                    V.tensor_scalar(neg[:, q], h[:, bass.ds(c * (step * D), step * D)], 0.0, None,
                                    ALU.min).then_inc(lowered, 1)

                lower(0, 0)
                lower(1, 1)

                def finish(c, q):
                    at = h[:, bass.ds(c * (step * D), step * D)]
                    dve.wait_ge(expd, c + 1)
                    V.scalar_tensor_tensor(out=at, in0=at, scalar=0.0, in1=neg[:, q],
                                           op0=ALU.max, op1=ALU.add).then_inc(done, 1)
                    dve.wait_ge(done, c + 1)

                with dve.Fori(0, chunks // 2 - 1) as i:
                    for q in range(2):
                        finish(i * 2 + q, q)
                        lower(i * 2 + (q + 2), q)
                for q in range(2):
                    finish(chunks - 2 + q, q)
                st.then(V.tensor_scalar(h[:], h[:], -1.0, None, ALU.add))

            @block.scalar
            def _(act):
                with act.Fori(0, chunks // 2) as i:
                    for q in range(2):
                        act.wait_ge(lowered, i * 2 + (q + 1))
                        nc.scalar.activation(neg[:, q], neg[:, q], ACT.Exp).then_inc(expd, 1)


def move(nc, stage, pairs):
    ctx, _, sem = scope(nc, stage)
    with ctx:
        moved = sem("moved")
        with nc.Block() as block:

            @block.sync
            def _(sp):
                for to, of in pairs:
                    sp.dma_start(to, of).then_inc(moved, 16)
                sp.wait_ge(moved, 16 * len(pairs))


def start_move(nc, to, of, moved):
    with nc.Block() as block:

        @block.sync
        def _(sp):
            sp.dma_start(to, of).then_inc(moved, 16)


def in_sbuf(t):
    return t[:].rearrange("p (b d) -> p b d", d=D)


def in_dram(t):
    return t.rearrange("(b p) d -> p b d", p=P)


def linear(nc, S, A, x, z):
    ctx, sb, sem = scope(nc, "linear")
    with ctx:
        weight = sb("weight", [P, 2, D])
        bias = sb("bias", [P, D])
        transposed_weight(nc, S, "linear_w", A["L1_ffn_weight"], weight)
        move(nc, "linear_b", [(bias[:], bc(A["L1_ffn_bias"].rearrange("(a d) -> a d", a=1), [P, D]))])

        def feed(V, dve, b, rows):
            return V.tensor_copy(rows[:], z[:, bass.ds(b * D, D)])

        def posts(sb, sem):
            return [sb(f"t{q}", [P, D]) for q in range(2)], sem("biased")

        def post(V, dve, b, out, q, local):
            t, biased = local
            V.tensor_tensor(t[q][:], out, bias[:], ALU.add).then_inc(biased, 1)
            dve.wait_ge(biased, b + 1)
            at = x[:, bass.ds(b * D, D)]
            return V.tensor_tensor(at, at, t[q][:], ALU.add)

        project(nc, S, "linear_p", weight, D, feed, post, posts)


def build(nc, A, out):
    ctx = ExitStack()
    with ctx:
        def sb(name, shape, dt=FP32, c=ctx):
            return c.enter_context(nc.sbuf_tensor(name, shape, dt))

        def dram(name, shape, dt=FP32):
            return nc.dram_tensor(name, shape, dt, kind="Internal").ap()

        S, T = Shared(), Tables()
        S.ident, S.ones, S.lower, S.row = (sb(n, [P, P]) for n in ("ident", "ones", "lower", "row"))
        S.ident_b, S.lower_b, S.row_b, S.zero_b = (
            sb(n, [P, P], BF16) for n in ("ident_b", "lower_b", "row_b", "zero_b"))
        S.col, S.minus_col, S.dinv = sb("col", [P, 1]), sb("minus_col", [P, 1]), sb("dinv", [P, NB])
        S.bank = [ctx.enter_context(nc.psum_tensor(f"bank{i}", [P, 512], FP32)) for i in range(8)]
        T.edges = [dram("edge_src", (EDGE_ROWS * P,), I32), dram("edge_dst", (EDGE_ROWS * P,), I32)]
        T.blk = dram("blk_table", (WL,), I32)
        T.x, T.feat = (dram(n, (N_PAD, D)) for n in ("x_table", "feat_table"))
        T.el = dram("el_table", (N_PAD, HEADS))
        T.acc = [dram(f"acc{k}", ((NB + 1) * P, D)) for k in range(GROUP)]
        h_cleared, h_in, acc_cleared, x_kept, feat_kept = (
            ctx.enter_context(nc.semaphore(n))
            for n in ("h_cleared", "h_in", "acc_cleared", "x_kept", "feat_kept"))
        constants(nc, S)
        with ExitStack() as edges:
            S.src_i, S.blk_row = sb("src_i", [P, WL], I32, edges), sb("blk_row", [1, WL], I32, edges)
            S.rel_b, S.lo_b, S.hi_b = (sb(n, [P, WL], BF16, edges) for n in ("rel_b", "lo_b", "hi_b"))
            M = Masks()
            M.keep_f, M.keep_b, M.open_f, M.open_b = (
                sb(n, [P, LINE], BF16, edges) for n in ("keep_f", "keep_b", "open_f", "open_b"))
            M.chain, M.join = (sb(n, [HEADS, 2, P], FP32, edges) for n in ("chain", "join"))
            h = sb("h", [P, NB * D], FP32, edges)
            with ExitStack() as part:
                zero = sb("zero", [P, D], FP32, part)
                S.key, S.src_m = (sb(n, [P, WL], FP32, part) for n in ("key", "src_m"))
                S.hi128_b = sb("hi128_b", [P, WL], BF16, part)
                with ExitStack() as one:
                    S.rel = sb("rel", [P, WL], FP32, one)
                    prep_edges(nc, S, T, A["src"], A["dst"])
                start_load(nc, A["x"], h, h_cleared, h_in)
                clear_accumulators(nc, T, zero, acc_cleared)
                segment_masks(nc, S, M)
                degrees(nc, S)
                arrived(nc, h_in, 32)
                normalise(nc, "ln0", h, h, S.dinv)
                gcn_scatter(nc, S, T, h, zero, acc_cleared)
            with ExitStack() as part:
                x = sb("x", [P, NB * D], FP32, part)
                gcn_out(nc, S, T, A, x, h)
                normalise(nc, "ln1", x, h)
                experts(nc, S, A, x, h)
                start_move(nc, in_dram(T.x), in_sbuf(x), x_kept)
                normalise(nc, "ln2", x, h)
                arrived(nc, x_kept, 16)
            with ExitStack() as part:
                acc = sb("acc", [P, max(NB * WROW, 2 * HEADS * LINE)], FP32, part)
                for layer in (1, 2):
                    gat_tables(nc, S, T, A, layer, h, acc, feat_kept)
                    with ExitStack() as of_layer:
                        score = sb(f"score{layer}", [P, WL * HEADS], FP32, of_layer)
                        gat_scores(nc, S, T, layer, acc, score)
                        arrived(nc, feat_kept, 16 * layer)
                        gat_softmax(nc, S, layer, M, score, acc)
                        gat_gather(nc, S, T, layer, score, acc)
                    gat_finish(nc, layer, acc, h)
            z = sb("z_end", [P, NB * D], FP32, edges)
            add_from_dram(nc, h, T.x)
            normalise(nc, "ln3", h, z)
            linear(nc, S, A, h, z)
            full = (NBLK - 1) * P
            move(nc, "store", [(out[0:full, :].rearrange("(b p) d -> p b d", p=P), in_sbuf(h)[:, 0:NBLK - 1]),
                               (out[full:N, :], in_sbuf(h)[0:TAIL, NBLK - 1])])


def add_from_dram(nc, x, table):
    ctx, _, sem = scope(nc, "add")
    with ctx:
        added = sem("added")
        with nc.Block() as block:

            @block.gpsimd
            def _(pool):
                pool.dma_start(in_sbuf(x), in_dram(table), accum_op=ALU.add).then_inc(added, 16)
                pool.wait_ge(added, 16)


_INS = ["x", "src", "dst", "L0_gnn_W", "L0_gnn_b", "L0_ffn_Wr", "L0_ffn_br", "L0_ffn_W1", "L0_ffn_b1", "L0_ffn_W2",
        "L0_ffn_b2", "L0_ffn_gamma", "L0_ffn_beta", "L1_gnn_W1", "L1_gnn_al1", "L1_gnn_ar1", "L1_gnn_W2",
        "L1_gnn_al2", "L1_gnn_ar2", "L1_ffn_weight", "L1_ffn_bias"]


def kernel(**inputs):
    import numpy as _np
    import concourse.bacc as _bacc
    from concourse import mybir as _mybir
    from concourse.bass_utils import run_bass_kernel_spmd as _run

    nc = _bacc.Bacc("TRN2", target_bir_lowering=False, num_devices=1)
    arrays, args = {}, {}
    for name in _INS:
        a = _np.ascontiguousarray(inputs[name])
        arrays[f"in_{name}_dram"] = a
        args[name] = nc.dram_tensor(f"in_{name}_dram", a.shape, _mybir.dt.from_np(a.dtype), kind="ExternalInput").ap()
    out = nc.dram_tensor("out_0_dram", (N, D), _mybir.dt.float32, kind="ExternalOutput").ap()
    build(nc, args, out)
    r = _run(nc, [arrays], core_ids=[0])
    return r.results[0]["out_0_dram"]
```
